# Optimizing a Trainium2 kernel written in Bass

```python
import numpy as np
import jax
import jax.numpy as jnp

def _softmax(x, axis=-1):
    return jax.nn.softmax(x, axis=axis)

def _gelu(x):
    return jax.nn.gelu(x, approximate=True)

def _silu(x):
    return jax.nn.silu(x)

def _sigmoid(x):
    return jax.nn.sigmoid(x)

def _layernorm(x, axis=-1, eps=1e-05):
    m = jnp.mean(x, axis=axis, keepdims=True)
    v = jnp.var(x, axis=axis, keepdims=True)
    return (x - m) / jnp.sqrt(v + eps)

def _scatter_add(tgt, idx, src, axis=0):
    return tgt.at[idx].add(src)

def _segment_sum(src, seg, n):
    return jax.ops.segment_sum(src, seg, n)
kernel_name = 'mk_cond_resid_d1_seqx_r2_9c6411'

def setup_inputs(seed: int=0):
    np.random.seed(seed)
    _w = jnp.asarray

    def _rec_inputs():
        import jax
        import jax.numpy as jnp
        _rk = jax.random.key(seed)
        x = -0.0002928 + 1 * jax.random.normal(jax.random.fold_in(_rk, 1), (2, 2048, 512), jnp.float32)
        _lenS = 2048 - jax.random.randint(jax.random.fold_in(_rk, 7), (2,), 0, max(1, 2048 // 4) + 1, jnp.int32)
        _lenS2 = 2048 - jax.random.randint(jax.random.fold_in(_rk, 8), (2,), 0, max(1, 2048 // 4) + 1, jnp.int32)
        fside_16xSxS_0 = -5.72187e-05 + 0.999849 * jax.random.normal(jax.random.fold_in(_rk, 11), (16, 2048, 2048), jnp.float32)
        cond_64 = -0.0265395 + 0.99382 * jax.random.normal(jax.random.fold_in(_rk, 13), (2, 64), jnp.float32)
        _validS = jnp.arange(2048)[None, :] < _lenS[:, None]
        _validS2 = jnp.arange(2048)[None, :] < _lenS2[:, None]
        _causal = jnp.tril(jnp.ones((2048, 2048), dtype=bool))
        mask_BxS_bk0 = jnp.logical_not(jnp.broadcast_to(_validS[:, :], (2, 2048)))
        return (x, fside_16xSxS_0, cond_64, mask_BxS_bk0)
    x, fside_16xSxS_0, cond_64, mask_BxS_bk0 = _rec_inputs()

    def _L0_cond_setup():
        import jax, jax.numpy as jnp
        import numpy as np
        B, N, DIM, H, DH = (2, 1024, 512, 16, 64)
        INNER = H * DH
        EPS = 1e-05

        def layernorm(x, g):
            mean = jnp.mean(x, axis=-1, keepdims=True)
            var = jnp.var(x, axis=-1, keepdims=True)
            return (x - mean) * jax.lax.rsqrt(var + EPS) * g
        key = jax.random.key(seed)
        ks = jax.random.split(key, 10)
        x = jax.random.normal(ks[0], (B, N, DIM), dtype=jnp.float32)
        attn_bias = jax.random.normal(ks[1], (H, N, N), dtype=jnp.float32)
        mask = jax.random.randint(ks[2], (B, N), 0, 2).astype(bool)
        g_in = jnp.ones((DIM,), dtype=jnp.float32)
        null_attn_bias = jax.random.normal(ks[3], (H,), dtype=jnp.float32)
        null_kv = jax.random.normal(ks[4], (2, DH), dtype=jnp.float32)
        Wq = jax.random.normal(ks[5], (DIM, INNER), dtype=jnp.float32) * 0.02
        Wkv = jax.random.normal(ks[6], (DIM, 2 * DH), dtype=jnp.float32) * 0.02
        Wo = jax.random.normal(ks[7], (INNER, DIM), dtype=jnp.float32) * 0.02
        g_out = jnp.ones((DIM,), dtype=jnp.float32)
        return {'x': x, 'attn_bias': attn_bias, 'mask': mask, 'g_in': g_in, 'null_attn_bias': null_attn_bias, 'null_kv': null_kv, 'Wq': Wq, 'Wkv': Wkv, 'Wo': Wo, 'g_out': g_out}
    _L0_cond_all = _L0_cond_setup()
    _L0_cond_in = {k: v for k, v in _L0_cond_all.items() if k in ('g_in', 'null_attn_bias', 'Wq', 'Wkv', 'Wo', 'g_out')}
    del _L0_cond_all
    return {'x': x, 'fside_16xSxS_0': fside_16xSxS_0, 'cond_64': cond_64, 'mask_BxS_bk0': mask_BxS_bk0, 'L0_cond_g_in': _L0_cond_in['g_in'], 'L0_cond_null_attn_bias': _L0_cond_in['null_attn_bias'], 'L0_cond_Wq': _L0_cond_in['Wq'], 'L0_cond_Wkv': _L0_cond_in['Wkv'], 'L0_cond_Wo': _L0_cond_in['Wo'], 'L0_cond_g_out': _L0_cond_in['g_out']}

def reference(x, fside_16xSxS_0, cond_64, mask_BxS_bk0, L0_cond_g_in, L0_cond_null_attn_bias, L0_cond_Wq, L0_cond_Wkv, L0_cond_Wo, L0_cond_g_out):
    import jax
    import jax.numpy as jnp

    def _L0_cond_ref(x, attn_bias, mask, g_in, null_attn_bias, null_kv, Wq, Wkv, Wo, g_out):
        import jax, jax.numpy as jnp
        import numpy as np
        B, N, DIM, H, DH = (2, 1024, 512, 16, 64)
        INNER = H * DH
        EPS = 1e-05

        def layernorm(x, g):
            mean = jnp.mean(x, axis=-1, keepdims=True)
            var = jnp.var(x, axis=-1, keepdims=True)
            return (x - mean) * jax.lax.rsqrt(var + EPS) * g
        b, n, _ = x.shape
        scale = DH ** (-0.5)
        xn = layernorm(x, g_in)
        q = (xn @ Wq).reshape(b, n, H, DH).transpose(0, 2, 1, 3) * scale
        kv = xn @ Wkv
        k, v = (kv[..., :DH], kv[..., DH:])
        nk = jnp.broadcast_to(null_kv[0], (b, 1, DH))
        nv = jnp.broadcast_to(null_kv[1], (b, 1, DH))
        k = jnp.concatenate([nk, k], axis=1)
        v = jnp.concatenate([nv, v], axis=1)
        sim = jnp.einsum('bhid,bjd->bhij', q, k)
        null_col = jnp.broadcast_to(null_attn_bias[:, None, None], (H, n, 1))
        bias = jnp.concatenate([null_col, attn_bias], axis=-1)
        sim = sim + bias
        neg = -jnp.finfo(sim.dtype).max
        j = n + 1
        causal_mask = jnp.triu(jnp.ones((n, j), dtype=bool), k=j - n + 1)
        sim = jnp.where(causal_mask, neg, sim)
        mask_p = jnp.pad(mask, ((0, 0), (1, 0)), constant_values=True)
        sim = jnp.where(mask_p[:, None, None, :], sim, neg)
        attn = jax.nn.softmax(sim, axis=-1)
        out = jnp.einsum('bhij,bjd->bhid', attn, v)
        out = out.transpose(0, 2, 1, 3).reshape(b, n, INNER)
        out = out @ Wo
        return layernorm(out, g_out)
    x = x + _L0_cond_ref(x, fside_16xSxS_0, mask_BxS_bk0, L0_cond_g_in, L0_cond_null_attn_bias, cond_64, L0_cond_Wq, L0_cond_Wkv, L0_cond_Wo, L0_cond_g_out)
    return x

_drawn_inputs = setup_inputs


def setup_inputs(seed=0):
    import zlib

    import numpy as np

    out = dict(_drawn_inputs(seed))
    spreads = {'L0_cond_g_in': (1.0, 0.2), 'L0_cond_g_out': (1.0, 0.2)}
    factors = {}
    for name, (base, spread) in spreads.items():
        noise = np.random.default_rng([zlib.crc32(name.encode()), seed]).standard_normal(out[name].shape)
        drawn = base * np.exp(spread * noise) if base else spread * noise
        out[name] = jnp.asarray(drawn.astype(out[name].dtype))
    for name, factor in factors.items():
        out[name] = (out[name] * factor).astype(out[name].dtype)
    return out
```

```python
from contextlib import ExitStack

import concourse.bass as bass
from concourse import mybir

F32 = mybir.dt.float32
F16 = mybir.dt.float16
ALU = mybir.AluOpType
ACT = mybir.ActivationFunctionType
AX_X = mybir.AxisListType.X
ABSMAX = bass.bass_isa.ReduceOp.absmax

P = 128
DH = 64
GROUP = 4
CHUNK = 1024
BODY = 8
EPS = 1e-5
FAR = 1e30
PSCALE = 16384.0
MASK_ONE, MASK_FAR = 32768.0, 60000.0


def cond_attention(nc, x, bias, cond, mask, g_in, null_bias, wq, wkv, wo, g_out, out):
    B, N, D = x.shape
    H = bias.shape[0]
    INNER = H * DH
    QT = N // P
    C = D // P
    CO = INNER // P
    STEPS = H * B
    TURNS = STEPS // BODY
    NSN = DH + H
    assert B == 2 and D == C * P and BODY == 4 * B and STEPS % BODY == 0

    with ExitStack() as ctx:
        def sb(name, shape, dt):
            return ctx.enter_context(nc.sbuf_tensor(name, shape, dt))

        def sem(name):
            return ctx.enter_context(nc.semaphore(name))

        ident = sb("ident", [P, P], F32)
        wqh = sb("wqh", [P, C, INNER], F16)
        wql = sb("wql", [P, C, INNER], F16)
        wkh = sb("wkh", [P, C, 2, DH], F16)
        wkl = sb("wkl", [P, C, 2, DH], F16)
        wvh = sb("wvh", [P, C, NSN], F16)
        wvl = sb("wvl", [P, C, NSN], F16)
        woh = sb("woh", [P, CO, D], F16)
        wol = sb("wol", [P, CO, D], F16)
        gcol = sb("gcol", [P, C], F32)
        gout = sb("gout", [P, D], F32)
        nv = sb("nv", [P, DH], F32)
        nb = sb("nb", [P, H], F32)
        maxes = sb("maxes", [P, 12], F32)
        allmax = sb("allmax", [P, 12], F32)
        sc = sb("sc", [P, 12], F32)
        powers = sb("powers", [P, 4], F32)
        k1 = sb("k1", [P, B, N], F16)
        k2 = sb("k2", [P, B, N], F16)
        v = sb("v", [P, QT, B, 2, DH], F16)
        xin = sb("xin", [P, B, D], F32)
        xres = sb("xres", [P, B, D], F32)
        xth = sb("xth", [P, C, B, P], F16)
        xtl = sb("xtl", [P, C, B, P], F16)
        qa = sb("qa", [P, 2, H, B, P], F16)
        qb = sb("qb", [P, 2, H, B, P], F16)
        st = sb("st", [P, B, 8], F32)
        xst = sb("xst", [P, B, 2], F32)
        yst = sb("yst", [P, B, 2], F32)
        bs = sb("bs", [P, 4, N], F32)
        ps = sb("ps", [P, 4, N], F32)
        pth = sb("pth", [P, 4, GROUP * P], F16)
        ptl = sb("ptl", [P, 4, GROUP * P], F16)
        rowmin = sb("rowmin", [P, BODY, 2], F32)
        start = sb("start", [P, BODY], F32)
        nsn = sb("nsn", [P, 3, B, H], F32)
        negm = sb("negm", [P, 2, B, H], F32)
        rsum = sb("rsum", [P, 2, 2, B, H], F32)
        pn = sb("pn", [P, B, H], F32)
        den = sb("den", [P, B, H], F32)
        att = sb("att", [P, B, H, DH], F32)
        nullv = sb("nullv", [P, H, DH], F32)
        ath = sb("ath", [P, B, CO, P], F16)
        atl = sb("atl", [P, B, CO, P], F16)
        y = sb("y", [P, B, D], F32)

        wq32 = bs[:, 0:2, :].rearrange("p a (c n) -> p (a c) n", n=INNER)
        wo32 = bs[:, 2:4, :].rearrange("p a (c n) -> p (a c) n", n=D)
        tmp = ps[:, 0:2, :].rearrange("p a (c n) -> p (a c) n", n=INNER)
        wkv32 = ps[:, 2, 0:C * 2 * DH].rearrange("p (c n) -> p c n", c=C)
        wn32 = ps[:, 3, 0:C * H].rearrange("p (c h) -> p c h", c=C)
        nk = ps[:, 3, C * H:C * H + DH]
        mask8 = ps[:, 3, N // 2:N].bitcast(mybir.dt.uint8).rearrange("p (b n) -> p b n", b=B)

        sp = ctx.enter_context(nc.psum_tensor("sp", [P, 2, CHUNK], F32))
        tp = ctx.enter_context(nc.psum_tensor("tp", [P, 2, 512], F32))
        op = ctx.enter_context(nc.psum_tensor("op", [P, 2, 512], F32))

        wq_in, wkv_in, wo_in = sem("wq_in"), sem("wkv_in"), sem("wo_in")
        small_in, mask_in = sem("small_in"), sem("mask_in")
        x_in, xres_in = sem("x_in"), sem("xres_in")
        bias_in = [sem(f"bias_in{k}") for k in range(4)]
        y_out = sem("y_out")
        ident_ready = sem("ident_ready")
        maxes_ready = sem("maxes_ready")
        allmax_ready = sem("allmax_ready")
        square_ready = sem("square_ready")
        root_ready = sem("root_ready")
        xvar_ready = sem("xvar_ready")
        xstd_ready = sem("xstd_ready")
        yvar_ready = sem("yvar_ready")
        ystd_ready = sem("ystd_ready")
        weights_ready = sem("weights_ready")
        dve_passed = sem("dve_passed")
        pool_passed = sem("pool_passed")
        dve_link = sem("dve_link")
        pool_link = sem("pool_link")
        xn_ready = sem("xn_ready")
        qb_ready = sem("qb_ready")
        unit_full = sem("unit_full")
        unit_high = sem("unit_high")
        unit_free = sem("unit_free")
        scores_full = sem("scores_full")
        biased = sem("biased")
        bias_ready = sem("bias_ready")
        start_ready = sem("start_ready")
        exp_done = sem("exp_done")
        pv_done = sem("pv_done")
        o_out = sem("o_out")
        null_shift = sem("null_shift")
        null_p = sem("null_p")
        den_ready = sem("den_ready")
        o_sum = sem("o_sum")
        att_ready = sem("att_ready")
        y_ready = sem("y_ready")
        def stand(eng, passed):
            eng.sem_inc(passed, 1)

        def bc(row, n):
            return row.rearrange("(a n) -> a n", a=1).broadcast_to([P, n])

        def span(i, n):
            return slice(i, i + n) if isinstance(i, int) else bass.ds(i, n)

        def blocks(t):
            return t + 1

        def groups(t):
            return [range(g, min(g + GROUP, t + 1)) for g in range(0, t + 1, GROUP)]

        def chunks(t):
            L = (t + 1) * P
            return [(c, min(c + CHUNK, L)) for c in range(0, L, CHUNK)]

        UX, UQ = B, H // 4
        UP = UX + UQ + 2
        UE = B * (CO // GROUP) + B

        pro_base, epi_base, loop_base = {0: 0}, {}, {}
        pro_high, epi_high, loop_high = {0: 0}, {}, {}
        u, hi, step_at, chunk_at, group_at, og_at = UP, UP, {}, {}, {}, {}
        nchunk = ngroup = 0
        for t in range(QT):
            if t + 1 < QT:
                pro_base[t + 1], pro_high[t + 1] = u, hi
                u, hi = u + UP, hi + UP
            if t > 0:
                epi_base[t - 1], epi_high[t - 1] = u, hi
                u, hi = u + UE, hi + UE - B
            loop_base[t], loop_high[t] = u, hi
            u, hi = u + STEPS * len(groups(t)), hi + STEPS * len(groups(t))
            step_at[t], og_at[t] = t * STEPS, t * STEPS // 4
            chunk_at[t], group_at[t] = nchunk, ngroup
            nchunk += STEPS * len(chunks(t))
            ngroup += STEPS * len(groups(t))
        epi_base[QT - 1], epi_high[QT - 1] = u, hi
        for t in range(QT):
            assert loop_base[t] % 2 == 0 and chunk_at[t] % 2 == 0 and group_at[t] % 4 == 0

        def more_all(it):
            return not isinstance(it, int) or it < TURNS - 1

        def s_places(t):
            return {0: 0, (2 if len(chunks(t)) > 1 else -1): len(chunks(t)) - 1}

        def head_loop(eng, t, window):
            if t == 0:
                for j in range(BODY):
                    window(0, j, True, True)
            with eng.Fori(int(t == 0), TURNS - 1) as it:
                for j in range(BODY):
                    window(it, j, True, True)
            for j in range(BODY):
                window(TURNS - 1, j, j + 2 < BODY, j + 1 < BODY)

        block = ctx.enter_context(nc.Block())

        @block.sync
        def _(eng):
            eng.dma_start(wkv32, wkv.rearrange("(c p) n -> p c n", p=P)).then_inc(wkv_in, 16)
            eng.dma_start(wq32, wq.rearrange("(c p) n -> p c n", p=P)).then_inc(wq_in, 16)
            eng.dma_start(xin[:, :, :], x[:, 0:P, :].rearrange("b p d -> p b d")).then_inc(x_in, 16)
            eng.dma_start(wo32, wo.rearrange("(c p) n -> p c n", p=P)).then_inc(wo_in, 16)

            def load_bias(t, it, k):
                L = (t + 1) * P
                if t > 0 or not isinstance(it, int) or it > 0:
                    if isinstance(it, int) and it == 0:
                        eng.wait_ge(biased, chunk_at[t - 1] + len(chunks(t - 1)) * (BODY * (TURNS - 1) + B * (k + 1)))
                    else:
                        eng.wait_ge(biased, chunk_at[t] + len(chunks(t)) * (BODY * (it - 1) + B * (k + 1)))
                eng.dma_start(bs[:, k, 0:L], bias[4 * it + k, t * P:(t + 1) * P, 0:L]).then_inc(bias_in[k], 16)

            eng.wait_ge(weights_ready, 1)
            for t in range(QT):
                for k in range(4):
                    load_bias(t, 0, k)
                if t + 1 < QT:
                    eng.wait_ge(unit_full, pro_base[t] + B)
                    eng.dma_start(xin[:, :, :], x[:, (t + 1) * P:(t + 2) * P, :].rearrange("b p d -> p b d")
                                  ).then_inc(x_in, 16)
                if t > 0:
                    if t > 1:
                        eng.wait_ge(y_ready, B * (t - 1))
                    eng.dma_start(xres[:, :, :], x[:, (t - 1) * P:t * P, :].rearrange("b p d -> p b d")
                                  ).then_inc(xres_in, 16)
                with eng.Fori(1, TURNS) as it:
                    for k in range(4):
                        load_bias(t, it, k)
                if t > 0:
                    eng.wait_ge(y_ready, B * t)
                    eng.dma_start(out[:, (t - 1) * P:t * P, :].rearrange("b p d -> p b d"), y[:, :, :]
                                  ).then_inc(y_out, 16)
            t = QT - 1
            eng.dma_start(xres[:, :, :], x[:, t * P:(t + 1) * P, :].rearrange("b p d -> p b d")).then_inc(xres_in, 16)
            eng.wait_ge(y_ready, B * QT)
            eng.dma_start(out[:, t * P:(t + 1) * P, :].rearrange("b p d -> p b d"), y[:, :, :]).then_inc(y_out, 16)
            eng.wait_ge(y_out, 16 * QT)

        @block.gpsimd
        def _(eng):
            links = [0]

            def link(ins):
                links[0] += 1
                ins.then_inc(pool_link, 1)
                eng.wait_ge(pool_link, links[0])

            nc.gpsimd.memset(powers[:, 0:1], 0.5)
            nc.gpsimd.memset(powers[:, 1:1 + B], -0.5)
            link(nc.gpsimd.memset(ident[:, :], 1.0))
            nc.gpsimd.affine_select(out=ident[:, :], in_=ident[:, :], pattern=[[-1, P]], compare_op=ALU.is_equal,
                                    fill=0.0, base=0, channel_multiplier=1).then_inc(ident_ready, 1)
            eng.wait_ge(maxes_ready, 1)
            nc.gpsimd.partition_all_reduce(allmax[:, :], maxes[:, :], P, ABSMAX).then_inc(allmax_ready, 1)

            far = eng.to_reg(-FAR)
            eng.wait_ge(square_ready, 1)
            nc.gpsimd.tensor_tensor(sc[:, 2:3], sc[:, 1:2], powers[:, 0:1], ALU.pow).then_inc(root_ready, 1)

            def inverse_std(a, eps):
                link(nc.gpsimd.tensor_scalar(a[:, :, 1], a[:, :, 1], eps, None, ALU.add))
                return nc.gpsimd.tensor_tensor(a[:, :, 1], a[:, :, 1], powers[:, 1:1 + B], ALU.pow)

            def x_std(t):
                eng.wait_ge(xvar_ready, t + 1)
                inverse_std(xst, EPS).then_inc(xstd_ready, 1)

            def edge(t, it, k):
                eng.wait_ge(bias_in[k], 16 * (TURNS * t + it + 1))
                stand(eng, pool_passed)
                d = bs[:, k, t * P:(t + 1) * P]
                nc.gpsimd.affine_select(out=d, in_=d, pattern=[[-1, P]], compare_op=ALU.is_ge, fill=far, base=0,
                                        channel_multiplier=1).then_inc(bias_ready, 1)

            def null_starts(t, it):
                nc.gpsimd.tensor_copy(start[:, :].rearrange("p (h b) -> p b h", b=B),
                                      nsn[:, t % 3, :, span(4 * it, 4)]).then_inc(start_ready, 1)

            def keep_maxima(t, it):
                eng.wait_ge(biased, chunk_at[t] + len(chunks(t)) * BODY * (it + 1))
                ck = len(chunks(t)) - 1
                return nc.gpsimd.tensor_copy(negm[:, t % 2, :, span(4 * it, 4)],
                                             rowmin[:, :, ck].rearrange("p (h b) -> p b h", b=B))

            def denominators(t):
                r = t % 2
                nc.gpsimd.tensor_tensor(pn[:, :, :], negm[:, r, :, :], nsn[:, t % 3, :, :], ALU.subtract
                                        ).then_inc(null_shift, 1)
                eng.wait_ge(null_p, t + 1)
                link(nc.gpsimd.tensor_tensor(den[:, :, :], pn[:, :, :], rsum[:, r, 0, :, :], ALU.add))
                if len(chunks(t)) > 1:
                    link(nc.gpsimd.tensor_tensor(den[:, :, :], den[:, :, :], rsum[:, r, 1, :, :], ALU.add))
                nc.gpsimd.tensor_scalar(den[:, :, :], den[:, :, :], PSCALE, None, ALU.mult).then_inc(den_ready, 1)
                for b in range(B):
                    link(nc.gpsimd.tensor_tensor(nullv[:, :, :], pn[:, b, :].unsqueeze(2).broadcast_to([P, H, DH]),
                                                 nv[:, :].unsqueeze(1).broadcast_to([P, H, DH]), ALU.mult))
                    if b == 0:
                        eng.wait_ge(o_out, og_at[t] + STEPS // 4)
                    ins = nc.gpsimd.tensor_tensor(att[:, b, :, :], att[:, b, :, :], nullv[:, :, :], ALU.add)
                    if b + 1 < B:
                        link(ins)
                    else:
                        ins.then_inc(o_sum, 1)

            def rows_out(t):
                eng.wait_ge(yvar_ready, t + 1)
                inverse_std(yst, sc[:, 8:9]).then_inc(ystd_ready, 1)
                for b in range(B):
                    eng.wait_ge(unit_free, epi_base[t] + UE - B + b + 1)
                    link(nc.gpsimd.tensor_tensor(y[:, b, :], y[:, b, :], gout[:, :], ALU.mult))
                    if b == 0:
                        eng.wait_ge(xres_in, 16 * (t + 1))
                    nc.gpsimd.tensor_tensor(y[:, b, :], y[:, b, :], xres[:, b, :], ALU.add).then_inc(y_ready, 1)

            x_std(0)
            for t in range(QT):
                eng.wait_ge(unit_free, pro_base[t] + UP)
                for k in range(2):
                    edge(t, 0, k)
                null_starts(t, 0)
                if t + 1 < QT:
                    x_std(t + 1)
                if t > 0:
                    denominators(t - 1)
                    rows_out(t - 1)

                def window(it, j, more_scores, more_exp):
                    if j % 2 == 0 and j < 4:
                        edge(t, it, j // 2 + 2)
                    elif j % 2 == 0 and more_all(it):
                        edge(t, it + 1, j // 2 - 2)
                    if j == 5:
                        if not more_all(it):
                            link(keep_maxima(t, it))
                        else:
                            keep_maxima(t, it)
                            null_starts(t, it + 1)

                head_loop(eng, t, window)
            denominators(QT - 1)
            rows_out(QT - 1)

        @block.tensor
        def _(eng):
            def unit(n):
                if not isinstance(n, int) or n >= 2:
                    eng.wait_ge(unit_free, n - 1)

            def products(dst, pairs):
                for i, (a, m) in enumerate(pairs):
                    ins = nc.tensor.matmul(dst, a, m, start=i == 0, stop=i == len(pairs) - 1, skip_group_check=True)
                return ins

            def prologue(t):
                u0 = pro_base[t]
                for b in range(B):
                    unit(u0 + b)
                    eng.wait_ge(xn_ready, B * t + b + 1)
                    for c in range(C):
                        ins = nc.tensor.transpose(tp[:, (u0 + b) % 2, c * P:(c + 1) * P],
                                                  xin[:, b, c * P:(c + 1) * P], ident[:, :])
                    ins.then_inc(unit_full, 1)
                eng.wait_ge(unit_free, u0 + B)
                if t == 0:
                    eng.wait_ge(weights_ready, 1)
                for n in range(UQ):
                    unit(u0 + UX + n)
                    for m in range(2):
                        w = slice((2 * n + m) * P, (2 * n + m + 1) * P)
                        ins = products(tp[:, (u0 + UX + n) % 2, m * B * P:(m + 1) * B * P],
                                       [(wqs[:, c, w], xs[:, c, :, :].rearrange("p b q -> p (b q)"))
                                        for c in range(C) for wqs, xs in ((wqh, xth), (wqh, xtl), (wql, xth))])
                    ins.then_inc(unit_full, 1)
                un = u0 + UX + UQ
                unit(un)
                products(tp[:, un % 2, 0:B * P],
                         [(ws[:, c, :, :].rearrange("p a d -> p (a d)"), xs[:, c, :, :].rearrange("p b q -> p (b q)"))
                          for c in range(C) for ws, xs in ((wkh, xth), (wkh, xtl), (wkl, xth))]
                         ).then_inc(unit_full, 1)
                un += 1
                unit(un)
                for b in range(B):
                    ins = products(tp[:, un % 2, b * P:b * P + NSN],
                                   [(xs[:, c, b, :], ws[:, c, :])
                                    for c in range(C) for ws, xs in ((wvh, xth), (wvh, xtl), (wvl, xth))])
                ins.then_inc(unit_full, 1)

            def epilogue(t):
                u0 = epi_base[t]
                eng.wait_ge(att_ready, t + 1)
                un = u0
                for b in range(B):
                    rows = att[:, b, :, :].rearrange("p h d -> p (h d)")
                    for c0 in range(0, CO, GROUP):
                        unit(un)
                        for c in range(c0, c0 + GROUP):
                            ins = nc.tensor.transpose(tp[:, un % 2, (c - c0) * P:(c - c0 + 1) * P],
                                                      rows[:, c * P:(c + 1) * P], ident[:, :])
                        ins.then_inc(unit_full, 1)
                        un += 1
                for b in range(B):
                    unit(un)
                    eng.wait_ge(unit_free, u0 + (b + 1) * (CO // GROUP))
                    products(tp[:, un % 2, 0:D],
                             [(a[:, b, c, :], w[:, c, :])
                              for c in range(CO) for a, w in ((ath, woh), (ath, wol), (atl, woh))]
                             ).then_inc(unit_full, 1)
                    un += 1

            def scores(t, it, j, ck):
                s = BODY * it + j
                h = 4 * it + j // 2
                lo, hi = chunks(t)[ck]
                n = chunk_at[t] + len(chunks(t)) * s + ck
                slot = (len(chunks(t)) * j + ck) % 2
                if t > 0 or j > 1 or not isinstance(it, int) or it > 0:
                    eng.wait_ge(biased, n - 1)
                for a in range(lo, hi, 512):
                    e = min(a + 512, hi)
                    dst = sp[:, slot, a - lo:e - lo]
                    nc.tensor.matmul(dst, qa[:, t % 2, h, j % 2, :], k1[:, j % 2, a:e], start=True, stop=False,
                                     skip_group_check=True)
                    ins = nc.tensor.matmul(dst, qb[0:DH + 1, t % 2, h, j % 2, :], k2[0:DH + 1, j % 2, a:e],
                                           start=False, stop=True, skip_group_check=True)
                ins.then_inc(scores_full, 1)

            def turn_p(t, it, j, g):
                G = len(groups(t))
                s = BODY * it + j
                n = loop_base[t] + G * s + g
                slot = (G * j + g) % 2
                unit(n)
                if g == 0:
                    eng.wait_ge(exp_done, chunk_at[t] + len(chunks(t)) * (s + 1))
                for i, kb in enumerate(groups(t)[g]):
                    ins = nc.tensor.transpose(tp[:, slot, i * P:(i + 1) * P],
                                              ps[:, j % 4, kb * P:(kb + 1) * P], ident[:, :])
                ins.then_inc(unit_full, 1)

            def times_v(t, it, j, g):
                G = len(groups(t))
                s = BODY * it + j
                eng.wait_ge(unit_free, loop_base[t] + G * s + g + 1)
                if g == 0 and j % 4 == 0 and (t > 0 or j > 4 or not isinstance(it, int) or it > 0):
                    eng.wait_ge(o_out, og_at[t] + 2 * it + j // 4 - 1)
                r = (G * j + g) % 4
                dst = op[:, j // 4, (j % 4) * DH:(j % 4 + 1) * DH]
                kbs = groups(t)[g]
                for i, kb in enumerate(kbs):
                    a = slice(i * P, (i + 1) * P)
                    first, last = kb == 0, kb == t
                    nc.tensor.matmul(dst, pth[:, r, a], v[:, kb, j % 2, 0, :], start=first, stop=False,
                                     skip_group_check=True)
                    nc.tensor.matmul(dst, pth[:, r, a], v[:, kb, j % 2, 1, :], start=False, stop=False,
                                     skip_group_check=True)
                    ins = nc.tensor.matmul(dst, ptl[:, r, a], v[:, kb, j % 2, 0, :], start=False, stop=last,
                                           skip_group_check=True)
                ins.then_inc(pv_done, 1)

            eng.wait_ge(ident_ready, 1)
            prologue(0)
            for t in range(QT):
                eng.wait_ge(qb_ready, t + 1)
                eng.wait_ge(unit_free, pro_base[t] + UP)
                for j in range(2):
                    for ck in range(len(chunks(t))):
                        scores(t, 0, j, ck)
                if t + 1 < QT:
                    prologue(t + 1)
                if t > 0:
                    epilogue(t - 1)

                def window(it, j, more_scores, more_exp):
                    G = len(groups(t))
                    for g in range(G):
                        turn_p(t, it, j, g)
                        if more_scores and g in s_places(t):
                            scores(t, it + (j + 2) // BODY, (j + 2) % BODY, s_places(t)[g])
                        if g > 0:
                            times_v(t, it, j, g - 1)
                    times_v(t, it, j, G - 1)

                head_loop(eng, t, window)
            epilogue(QT - 1)

        @block.scalar
        def _(eng):
            def small(dst, src):
                eng.dma_start(dst, src).then_inc(small_in, 16)

            small(gcol[:, :], g_in)
            small(nk[:, :], bc(cond[0], DH))
            small(nv[:, :], bc(cond[1], DH))
            small(nb[:, :], bc(null_bias, H))
            small(gout[:, :], bc(g_out, D))
            eng.dma_start(mask8[DH:DH + 1, :, :], mask.rearrange("(a b) n -> a b n", a=1)).then_inc(mask_in, 16)

            def high(dst, src, scale=1.0):
                return nc.scalar.activation(dst, src, ACT.Copy, scale=scale)

            def prologue(t):
                u0, n = pro_base[t], pro_base[t]
                for b in range(B):
                    eng.wait_ge(unit_full, n + 1)
                    high(xth[:, :, b, :], tp[:, n % 2, :].rearrange("p (c q) -> p c q", c=C)).then_inc(unit_high, 1)
                    n += 1
                for i in range(UQ):
                    eng.wait_ge(unit_full, n + 1)
                    for odd in range(2):
                        ins = high(qa[0:DH, t % 2, 4 * i + odd:4 * i + odd + 3:2, :, :],
                                   tp[DH * odd:DH * odd + DH, n % 2, :].rearrange("p (m b q) -> p m b q", m=2, b=B))
                    ins.then_inc(unit_high, 1)
                    n += 1
                eng.wait_ge(unit_full, n + 1)
                high(k1[:, :, t * P:(t + 1) * P], tp[:, n % 2, 0:B * P].rearrange("p (b q) -> p b q", b=B)
                     ).then_inc(unit_high, 1)
                n += 1
                eng.wait_ge(unit_full, n + 1)
                high(v[:, t, :, 0, :], tp[:, n % 2, 0:B * P].rearrange("p (b q) -> p b q", b=B)[:, :, 0:DH]
                     ).then_inc(unit_high, 1)

            def epilogue(t):
                eng.wait_ge(null_shift, t + 1)
                nc.scalar.activation(pn[:, :, :], pn[:, :, :], ACT.Exp).then_inc(null_p, 1)
                n = epi_base[t]
                for b in range(B):
                    for c0 in range(0, CO, GROUP):
                        eng.wait_ge(unit_full, n + 1)
                        high(ath[:, b, c0:c0 + GROUP, :], tp[:, n % 2, :].rearrange("p (c q) -> p c q", c=GROUP)
                             ).then_inc(unit_high, 1)
                        n += 1

            def exp(t, it, j, ck):
                s = BODY * it + j
                h = 4 * it + j // 2
                if ck == 0:
                    eng.wait_ge(biased, chunk_at[t] + len(chunks(t)) * (s + 1))
                lo, hi = chunks(t)[ck]
                nc.scalar.activation(ps[:, j % 4, lo:hi], ps[:, j % 4, lo:hi], ACT.Exp,
                                     bias=rowmin[:, j, len(chunks(t)) - 1:len(chunks(t))], scale=-1.0,
                                     accum_out=rsum[:, t % 2, ck, j % 2, span(h, 1)]).then_inc(exp_done, 1)

            def p_high(t, it, j, g):
                G = len(groups(t))
                s = BODY * it + j
                eng.wait_ge(unit_full, loop_base[t] + G * s + g + 1)
                if t > 0 or G * j + g >= 4 or not isinstance(it, int) or it > 0:
                    eng.wait_ge(pv_done, group_at[t] + G * s + g - 3)
                w = len(groups(t)[g]) * P
                high(pth[:, (G * j + g) % 4, 0:w], tp[:, (G * j + g) % 2, 0:w], PSCALE).then_inc(unit_high, 1)

            prologue(0)
            for t in range(QT):
                for ck in range(len(chunks(t))):
                    exp(t, 0, 0, ck)
                if t + 1 < QT:
                    prologue(t + 1)
                if t > 0:
                    epilogue(t - 1)

                def window(it, j, more_scores, more_exp):
                    G = len(groups(t))
                    for g in range(G):
                        p_high(t, it, j, g)
                        if more_exp and g < len(chunks(t)):
                            exp(t, it + (j + 1) // BODY, (j + 1) % BODY, g)

                head_loop(eng, t, window)
            epilogue(QT - 1)

        @block.vector
        def _(eng):
            links = [0]

            def link(ins):
                links[0] += 1
                ins.then_inc(dve_link, 1)
                eng.wait_ge(dve_link, links[0])

            def low(dst, src, hi_half, scale=1.0):
                return nc.vector.scalar_tensor_tensor(out=dst, in0=src, scalar=scale, in1=hi_half, op0=ALU.mult,
                                                      op1=ALU.subtract)

            def setup():
                nc.vector.memset(maxes[:, :], 0.0)
                nc.vector.memset(rowmin[:, :, :], 0.0)
                eng.wait_ge(small_in, 16 * 5)
                eng.wait_ge(wkv_in, 16)
                for c in range(C):
                    nc.vector.tensor_scalar(wkv32[:, c, :], wkv32[:, c, :], gcol[:, c:c + 1], None, ALU.mult)
                eng.wait_ge(wq_in, 16)
                for c in range(C):
                    ins = nc.vector.tensor_scalar(wq32[:, c, :], wq32[:, c, :], gcol[:, c:c + 1], None, ALU.mult)
                link(ins)
                for c in range(C):
                    ins = nc.vector.scalar_tensor_tensor(
                        out=tmp[:, c, :].rearrange("p (h d) -> p h d", d=DH),
                        in0=wq32[:, c, :].rearrange("p (h d) -> p h d", d=DH), scalar=DH ** -0.5,
                        in1=nk[:, :].unsqueeze(1).broadcast_to([P, H, DH]), op0=ALU.mult, op1=ALU.mult)
                link(ins)
                for c in range(C):
                    ins = nc.vector.tensor_reduce(wn32[:, c, :], tmp[:, c, :].rearrange("p (h d) -> p h d", d=DH),
                                                  AX_X, ALU.add)
                link(ins)

                def largest(k, a):
                    nc.vector.tensor_reduce(maxes[:, k:k + 1], a, mybir.AxisListType.XY, ALU.max)
                    return nc.vector.tensor_reduce(maxes[:, 6 + k:7 + k], a, mybir.AxisListType.XY, ALU.min)

                largest(0, wq32)
                largest(1, wkv32[:, :, 0:DH])
                largest(2, wkv32[:, :, DH:2 * DH])
                largest(3, wn32)
                eng.wait_ge(wo_in, 16)
                largest(4, wo32)
                largest(5, nv[:, :].unsqueeze(1)).then_inc(maxes_ready, 1)
                eng.wait_ge(allmax_ready, 1)

                def col(k):
                    return sc[:, k:k + 1]

                link(nc.vector.scalar_tensor_tensor(out=allmax[:, 0:6], in0=allmax[:, 0:6], scalar=1e-18,
                                                    in1=allmax[:, 6:12], op0=ALU.max, op1=ALU.max))
                aq, ak, av, an, aw, anv = (allmax[:, k:k + 1] for k in range(6))
                link(nc.vector.reciprocal(col(0), ak))
                nc.vector.tensor_scalar(col(1), col(0), aq, DH ** -0.5, ALU.mult, ALU.mult).then_inc(square_ready, 1)
                eng.wait_ge(root_ready, 1)
                link(nc.vector.reciprocal(col(3), col(2)))
                nc.vector.tensor_scalar(col(3), col(3), DH ** -0.5, None, ALU.mult)
                link(nc.vector.tensor_scalar(col(4), anv, 1.0 / D, av, ALU.mult, ALU.max))
                link(nc.vector.reciprocal(col(4), col(4)))
                nc.vector.tensor_scalar(col(4), col(4), 16.0, None, ALU.mult)
                link(nc.vector.reciprocal(col(5), an))
                nc.vector.tensor_scalar(col(5), col(5), 16.0, None, ALU.mult)
                nc.vector.tensor_scalar(col(6), an, -1.0 / 16.0, None, ALU.mult)
                link(nc.vector.reciprocal(col(7), aw))
                link(nc.vector.tensor_scalar(col(7), col(7), 1024.0, None, ALU.mult))
                link(nc.vector.tensor_scalar(col(8), col(4), col(7), None, ALU.mult))
                link(nc.vector.tensor_scalar(col(8), col(8), col(8), EPS, ALU.mult, ALU.mult))
                nc.vector.tensor_scalar(nv[:, :], nv[:, :], col(4), PSCALE, ALU.mult, ALU.mult)
                nc.vector.tensor_scalar(wq32, wq32, col(3), None, ALU.mult)
                nc.vector.tensor_scalar(wo32, wo32, col(7), None, ALU.mult)
                nc.vector.tensor_scalar(wkv32[:, :, 0:DH], wkv32[:, :, 0:DH], col(2), None, ALU.mult)
                nc.vector.tensor_scalar(wkv32[:, :, DH:2 * DH], wkv32[:, :, DH:2 * DH], col(4), None, ALU.mult)
                link(nc.vector.tensor_scalar(wn32, wn32, col(5), None, ALU.mult))
                nc.vector.tensor_copy(wqh[:, :, :], wq32)
                nc.vector.tensor_copy(woh[:, :, :], wo32)
                for a in range(2):
                    nc.vector.tensor_copy(wkh[:, :, a, :], wkv32[:, :, 0:DH])
                nc.vector.tensor_copy(wvh[:, :, 0:DH], wkv32[:, :, DH:2 * DH])
                link(nc.vector.tensor_copy(wvh[:, :, DH:NSN], wn32))
                nc.vector.tensor_tensor(wql[:, :, :], wq32, wqh[:, :, :], ALU.subtract)
                nc.vector.tensor_tensor(wol[:, :, :], wo32, woh[:, :, :], ALU.subtract)
                for a in range(2):
                    nc.vector.tensor_tensor(wkl[:, :, a, :], wkv32[:, :, 0:DH], wkh[:, :, a, :], ALU.subtract)
                nc.vector.tensor_tensor(wvl[:, :, 0:DH], wkv32[:, :, DH:2 * DH], wvh[:, :, 0:DH], ALU.subtract)
                nc.vector.tensor_tensor(wvl[:, :, DH:NSN], wn32, wvh[:, :, DH:NSN], ALU.subtract)
                nc.vector.memset(qb[DH:DH + 1, :, :, :, :], MASK_ONE)
                eng.wait_ge(mask_in, 16)
                nc.vector.tensor_scalar(k2[DH:DH + 1, :, :], mask8[DH:DH + 1, :, :], -1.0, MASK_FAR, ALU.add,
                                        ALU.mult).then_inc(weights_ready, 1)

            def moments(dst, b, src):
                link(nc.vector.bn_stats(st[:, b, 0:6], src))
                return nc.vector.bn_aggr(dst[:, b, :], st[:, b, 0:6])

            def norm_x(t):
                eng.wait_ge(x_in, 16 * (t + 1))
                for b in range(B):
                    ins = moments(xst, b, xin[:, b, :])
                ins.then_inc(xvar_ready, 1)
                eng.wait_ge(xstd_ready, t + 1)
                for b in range(B):
                    nc.vector.tensor_scalar(xin[:, b, :], xin[:, b, :], xst[:, b, 0:1], xst[:, b, 1:2], ALU.subtract,
                                            ALU.mult).then_inc(xn_ready, 1)

            def prologue(t):
                n, h = pro_base[t], pro_high[t]
                for b in range(B):
                    eng.wait_ge(unit_high, h + 1)
                    low(xtl[:, :, b, :], tp[:, n % 2, :].rearrange("p (c q) -> p c q", c=C), xth[:, :, b, :]
                        ).then_inc(unit_free, 1)
                    n, h = n + 1, h + 1
                for i in range(UQ):
                    eng.wait_ge(unit_high, h + 1)
                    for odd in range(2):
                        hs = slice(4 * i + odd, 4 * i + odd + 3, 2)
                        ins = low(qa[DH:P, t % 2, hs, :, :],
                                  tp[DH * odd:DH * odd + DH, n % 2, :].rearrange("p (m b q) -> p m b q", m=2, b=B),
                                  qa[0:DH, t % 2, hs, :, :])
                    ins.then_inc(unit_free, 1)
                    n, h = n + 1, h + 1
                nc.vector.tensor_copy(qb[0:DH, t % 2, :, :, :], qa[0:DH, t % 2, :, :, :]).then_inc(qb_ready, 1)
                eng.wait_ge(unit_high, h + 1)
                low(k2[0:DH, :, t * P:(t + 1) * P], tp[0:DH, n % 2, 0:B * P].rearrange("p (b q) -> p b q", b=B),
                    k1[0:DH, :, t * P:(t + 1) * P]).then_inc(unit_free, 1)
                n, h = n + 1, h + 1
                eng.wait_ge(unit_high, h + 1)
                vals = tp[:, n % 2, 0:B * P].rearrange("p (b q) -> p b q", b=B)
                low(v[:, t, :, 1, :], vals[:, :, 0:DH], v[:, t, :, 0, :])
                nc.vector.scalar_tensor_tensor(
                    out=nsn[:, t % 3, :, :], in0=vals[:, :, DH:NSN], scalar=sc[:, 6:7],
                    in1=nb[:, :].unsqueeze(1).broadcast_to([P, B, H]), op0=ALU.mult, op1=ALU.subtract
                ).then_inc(unit_free, 1)

            def epilogue(t):
                eng.wait_ge(den_ready, t + 1)
                link(nc.vector.reciprocal(den[:, :, :], den[:, :, :]))
                eng.wait_ge(o_sum, t + 1)
                nc.vector.tensor_tensor(att[:, :, :, :], att[:, :, :, :],
                                        den[:, :, :].unsqueeze(3).broadcast_to([P, B, H, DH]), ALU.mult
                                        ).then_inc(att_ready, 1)
                n, h = epi_base[t], epi_high[t]
                for b in range(B):
                    for c0 in range(0, CO, GROUP):
                        eng.wait_ge(unit_high, h + 1)
                        low(atl[:, b, c0:c0 + GROUP, :], tp[:, n % 2, :].rearrange("p (c q) -> p c q", c=GROUP),
                            ath[:, b, c0:c0 + GROUP, :]).then_inc(unit_free, 1)
                        n, h = n + 1, h + 1
                if t > 0:
                    eng.wait_ge(y_out, 16 * t)
                for b in range(B):
                    eng.wait_ge(unit_full, n + b + 1)
                    ins = moments(yst, b, tp[:, (n + b) % 2, 0:D])
                ins.then_inc(yvar_ready, 1)
                eng.wait_ge(ystd_ready, t + 1)
                for b in range(B):
                    nc.vector.tensor_scalar(y[:, b, :], tp[:, (n + b) % 2, 0:D], yst[:, b, 0:1], yst[:, b, 1:2],
                                            ALU.subtract, ALU.mult).then_inc(unit_free, 1)

            def add_bias(t, it, j, ck):
                s = BODY * it + j
                k = j // 2
                n = chunk_at[t] + len(chunks(t)) * s + ck
                eng.wait_ge(scores_full, n + 1)
                if ck == 0:
                    if j % 2 == 0:
                        eng.wait_ge(bias_ready, H * t + 4 * it + k + 1)
                    if j == 0:
                        eng.wait_ge(start_ready, TURNS * t + it + 1)
                    first = start[:, j:j + 1]
                else:
                    eng.wait_ge(biased, n)
                    first = rowmin[:, j, ck - 1:ck]
                stand(eng, dve_passed)
                lo, hi = chunks(t)[ck]
                slot = (len(chunks(t)) * j + ck) % 2
                nc.vector.tensor_tensor_reduce(ps[:, j % 4, lo:hi], sp[:, slot, 0:hi - lo], bs[:, k, lo:hi], -1.0,
                                               first, ALU.add, ALU.min, rowmin[:, j, ck:ck + 1]
                                               ).then_inc(biased, 1)

            def p_low(t, it, j, g):
                G = len(groups(t))
                s = BODY * it + j
                eng.wait_ge(unit_high, loop_high[t] + G * s + g + 1)
                w = len(groups(t)[g]) * P
                r = (G * j + g) % 4
                low(ptl[:, r, 0:w], tp[:, (G * j + g) % 2, 0:w], pth[:, r, 0:w], PSCALE).then_inc(unit_free, 1)

            def take_o(t, it, j):
                G = len(groups(t))
                eng.wait_ge(pv_done, group_at[t] + G * (BODY * it + j + 1))
                h = 4 * it + 2 * (j // 4)
                for b in range(B):
                    ins = nc.vector.tensor_copy(
                        att[:, b, span(h, 2), :],
                        op[:, j // 4, 0:4 * DH].rearrange("p (h b d) -> p h b d", h=2, b=B)[:, :, b, :])
                ins.then_inc(o_out, 1)

            setup()
            norm_x(0)
            prologue(0)
            for t in range(QT):
                for j in range(2):
                    for ck in range(len(chunks(t))):
                        add_bias(t, 0, j, ck)
                if t + 1 < QT:
                    norm_x(t + 1)
                    prologue(t + 1)
                if t > 0:
                    epilogue(t - 1)

                def window(it, j, more_scores, more_exp):
                    for g in range(len(groups(t))):
                        p_low(t, it, j, g)
                        if more_scores and g in s_places(t):
                            add_bias(t, it + (j + 2) // BODY, (j + 2) % BODY, s_places(t)[g])
                    if j % 4 == 3:
                        take_o(t, it, j)

                head_loop(eng, t, window)
            epilogue(QT - 1)


_INS = ['x', 'fside_16xSxS_0', 'cond_64', 'mask_BxS_bk0', 'L0_cond_g_in', 'L0_cond_null_attn_bias', 'L0_cond_Wq',
        'L0_cond_Wkv', 'L0_cond_Wo', 'L0_cond_g_out']


def kernel(**inputs):
    import numpy as np
    import concourse.bacc as bacc
    from concourse.bass_utils import run_bass_kernel_spmd

    nc = bacc.Bacc("TRN2", target_bir_lowering=False, num_devices=1)
    arrays, args = {}, []
    for name in _INS:
        a = np.ascontiguousarray(inputs[name])
        if name == 'L0_cond_g_in':
            a = np.ascontiguousarray(a.reshape(-1, P).T)
        arrays[f"in_{name}"] = a
        args.append(nc.dram_tensor(f"in_{name}", a.shape, mybir.dt.from_np(a.dtype), kind="ExternalInput").ap())
    out = nc.dram_tensor("out", arrays["in_x"].shape, F32, kind="ExternalOutput").ap()
    cond_attention(nc, *args, out)
    r = run_bass_kernel_spmd(nc, [arrays], core_ids=[0])
    return r.results[0]["out"]
```

```python
from contextlib import ExitStack

import concourse.bass as bass
from concourse import mybir

F32 = mybir.dt.float32
F16 = mybir.dt.float16
ALU = mybir.AluOpType
ACT = mybir.ActivationFunctionType
AX_X = mybir.AxisListType.X
ABSMAX = bass.bass_isa.ReduceOp.absmax

P = 128
DH = 64
GROUP = 4
CHUNK = GROUP * P
EXP = 2 * CHUNK
AHEAD = 3
SCORES_AHEAD = 2
TP = 4
BODY = 8
EPS = 1e-5
FAR = 1e30
PSCALE = 16384.0
MASK_ONE, MASK_FAR = 32768.0, 60000.0


def cond_attention(nc, x, bias, cond, mask, g_in, null_bias, wq, wkv, wo, g_out, out):
    B, N, D = x.shape
    H = bias.shape[0]
    INNER = H * DH
    QT = N // P
    C = D // P
    CO = INNER // P
    STEPS = H * B
    TURNS = STEPS // BODY
    NSN = DH + H
    assert B == 2 and D == C * P and BODY == 4 * B and STEPS % BODY == 0

    with ExitStack() as ctx:
        def sb(name, shape, dt):
            return ctx.enter_context(nc.sbuf_tensor(name, shape, dt))

        def sem(name):
            return ctx.enter_context(nc.semaphore(name))

        ident = sb("ident", [P, P], F32)
        wqh = sb("wqh", [P, C, INNER], F16)
        wql = sb("wql", [P, C, INNER], F16)
        wkh = sb("wkh", [P, C, 2, DH], F16)
        wkl = sb("wkl", [P, C, 2, DH], F16)
        wvh = sb("wvh", [P, C, NSN], F16)
        wvl = sb("wvl", [P, C, NSN], F16)
        woh = sb("woh", [P, CO, D], F16)
        wol = sb("wol", [P, CO, D], F16)
        gcol = sb("gcol", [P, C], F32)
        gout = sb("gout", [P, D], F32)
        nv = sb("nv", [P, DH], F32)
        nb = sb("nb", [P, H], F32)
        maxes = sb("maxes", [P, 12], F32)
        allmax = sb("allmax", [P, 12], F32)
        sc = sb("sc", [P, 12], F32)
        powers = sb("powers", [P, 4], F32)
        k1 = sb("k1", [P, B, N], F16)
        k2 = sb("k2", [P, B, N], F16)
        v = sb("v", [P, QT, B, 2, DH], F16)
        xin = sb("xin", [P, B, D], F32)
        xres = sb("xres", [P, B, D], F32)
        xth = sb("xth", [P, C, B, P], F16)
        xtl = sb("xtl", [P, C, B, P], F16)
        qa = sb("qa", [P, 2, H, B, P], F16)
        qb = sb("qb", [P, 2, H, B, P], F16)
        st = sb("st", [P, B, 8], F32)
        xst = sb("xst", [P, B, 2], F32)
        yst = sb("yst", [P, B, 2], F32)
        bs = sb("bs", [P, 2 * N], F32)
        ps = sb("ps", [P, 4, N], F32)
        pth = sb("pth", [P, 4, GROUP * P], F16)
        ptl = sb("ptl", [P, 4, GROUP * P], F16)
        rowmin = sb("rowmin", [P, BODY, 4], F32)
        start = sb("start", [P, BODY], F32)
        nsn = sb("nsn", [P, 3, B, H], F32)
        negm = sb("negm", [P, 2, B, H], F32)
        rsum = sb("rsum", [P, 2, 2, B, H], F32)
        pn = sb("pn", [P, B, H], F32)
        den = sb("den", [P, B, H], F32)
        att = sb("att", [P, 2, B, H, DH], F32)
        nullv = sb("nullv", [P, H, DH], F32)
        ath = sb("ath", [P, B, CO, P], F16)
        atl = sb("atl", [P, B, CO, P], F16)
        y = sb("y", [P, B, D], F32)

        wq32 = bs[:, :].rearrange("p (c n) -> p c n", n=INNER)
        wo32 = qa[:, :, :, :, :].rearrange("p a h b q -> p (a h b q)").bitcast(F32).rearrange("p (c n) -> p c n", n=D)
        tmp = ps[:, 0:2, :].rearrange("p a (c n) -> p (a c) n", n=INNER)
        wkv32 = ps[:, 2, 0:C * 2 * DH].rearrange("p (c n) -> p c n", c=C)
        wn32 = ps[:, 3, 0:C * H].rearrange("p (c h) -> p c h", c=C)
        nk = ps[:, 3, C * H:C * H + DH]
        mask8 = ps[:, 3, N // 2:N].bitcast(mybir.dt.uint8).rearrange("p (b n) -> p b n", b=B)

        sp = ctx.enter_context(nc.psum_tensor("sp", [P, 2, CHUNK], F32))
        tp = ctx.enter_context(nc.psum_tensor("tp", [P, TP, 512], F32))
        op = ctx.enter_context(nc.psum_tensor("op", [P, 2, 512], F32))

        wq_in, wkv_in, wo_in = sem("wq_in"), sem("wkv_in"), sem("wo_in")
        small_in, mask_in = sem("small_in"), sem("mask_in")
        x_in, xres_in = sem("x_in"), sem("xres_in")
        bias_in = [sem(f"bias_in{k}") for k in range(4)]
        y_out = sem("y_out")
        ident_ready = sem("ident_ready")
        maxes_ready = sem("maxes_ready")
        allmax_ready = sem("allmax_ready")
        square_ready = sem("square_ready")
        root_ready = sem("root_ready")
        xvar_ready = sem("xvar_ready")
        xstd_ready = sem("xstd_ready")
        yvar_ready = sem("yvar_ready")
        ystd_ready = sem("ystd_ready")
        weights_ready = sem("weights_ready")
        dve_passed = sem("dve_passed")
        pool_passed = sem("pool_passed")
        dve_link = sem("dve_link")
        pool_link = sem("pool_link")
        xn_ready = sem("xn_ready")
        qb_ready = sem("qb_ready")
        unit_full = sem("unit_full")
        unit_high = sem("unit_high")
        unit_free = sem("unit_free")
        scores_full = sem("scores_full")
        biased = sem("biased")
        bias_ready = sem("bias_ready")
        start_ready = sem("start_ready")
        exp_done = sem("exp_done")
        pv_done = sem("pv_done")
        o_out = sem("o_out")
        null_shift = sem("null_shift")
        null_p = sem("null_p")
        den_ready = sem("den_ready")
        o_sum = sem("o_sum")
        att_ready = sem("att_ready")
        y_ready = sem("y_ready")
        def stand(eng, passed):
            eng.sem_inc(passed, 1)

        def bc(row, n):
            return row.rearrange("(a n) -> a n", a=1).broadcast_to([P, n])

        def span(i, n):
            return slice(i, i + n) if isinstance(i, int) else bass.ds(i, n)

        def blocks(t):
            return t + 1

        def groups(t):
            return [range(g, min(g + GROUP, t + 1)) for g in range(0, t + 1, GROUP)]

        def chunk(t, ck, width=CHUNK):
            return ck * width, min((ck + 1) * width, (t + 1) * P)

        def exps(t):
            return -(-(t + 1) * P // EXP)

        def lead(t):
            return 2 if len(groups(t)) == 1 else 1

        def scored(t):
            G = len(groups(t))
            return min(2 * G + SCORES_AHEAD, 3 * G + 1)

        def bias_slots(t):
            return 4 if 4 * (t + 1) * P <= 2 * N else 2

        def early_edges(t):
            return -(-(AHEAD + scored(t)) // (B * len(groups(t))))

        def bias_row(t, h, a, e):
            at = (h % bias_slots(t)) * (2 * N // bias_slots(t))
            return bs[:, at + a:at + e]

        UX, UQ = B, H // 4
        UP = UX + UQ + 2
        UE = B * (CO // GROUP) + B

        pro_base, epi_base, loop_base, last_base = {0: 0}, {}, {}, {}
        pro_high, epi_high, loop_high, last_high = {0: 0}, {}, {}, {}
        u, hi, group_at, exp_at, bias_at = UP, UP, {}, {}, {}
        ngroup = nexp = 0
        uses = [0] * 4
        for t in range(QT):
            G = len(groups(t))
            loop_base[t], loop_high[t] = u, hi
            n = BODY * G * (TURNS - 1) + AHEAD
            u, hi = u + n, hi + n
            if t + 1 < QT:
                pro_base[t + 1], pro_high[t + 1] = u, hi
                u, hi = u + UP, hi + UP
            if t > 0:
                epi_base[t - 1], epi_high[t - 1] = u, hi
                u, hi = u + UE, hi + UE - B
            last_base[t], last_high[t] = u - n, hi - n
            u, hi = u + STEPS * G - n, hi + STEPS * G - n
            group_at[t], exp_at[t], bias_at[t] = ngroup, nexp, list(uses)
            ngroup += STEPS * G
            nexp += STEPS * exps(t)
            for k in range(bias_slots(t)):
                uses[k] += H // bias_slots(t)
        epi_base[QT - 1], epi_high[QT - 1] = u, hi

        def locate(t, it, f):
            G = len(groups(t))
            it, f = it + f // (BODY * G), f % (BODY * G)
            return it, f, f // G, f % G

        def here(it, f, t):
            return not isinstance(it, int) or locate(t, it, f)[0] < TURNS

        def unit_base(it, f, early, last):
            return early if not isinstance(it, int) or it < TURNS - 1 or f < AHEAD else last

        def unit_of(t, it, f):
            return unit_base(it, f, loop_base[t], last_base[t]) + BODY * len(groups(t)) * it + f

        def high_of(t, it, f):
            return unit_base(it, f, loop_high[t], last_high[t]) + BODY * len(groups(t)) * it + f

        def slot_of(t, it, f):
            return (unit_base(it, f, loop_base[t], last_base[t]) + f) % TP

        def group_of(t, it, f):
            return group_at[t] + BODY * len(groups(t)) * it + f

        def tile_loop(eng, t, first, turn, between):
            first()
            if t == 0:
                turn(0)
            with eng.Fori(int(t == 0), TURNS - 1) as it:
                turn(it)
            between()
            turn(TURNS - 1)

        def look_ahead(t, it, take, take_next):
            G = len(groups(t))
            ahead = AHEAD + scored(t)

            def at(f):
                if here(it, f + ahead, t):
                    take(*locate(t, it, f + ahead)[0:2])
                elif t + 1 < QT:
                    n = f + ahead - BODY * G
                    todo = scored(t + 1)
                    if n < todo:
                        take_next(n)
                    if f == BODY * G - 1:
                        for m in range(n + 1, todo):
                            take_next(m)
            return at

        block = ctx.enter_context(nc.Block())

        @block.sync
        def _(eng):
            eng.dma_start(wkv32, wkv.rearrange("(c p) n -> p c n", p=P)).then_inc(wkv_in, 16)
            eng.dma_start(wq32, wq.rearrange("(c p) n -> p c n", p=P)).then_inc(wq_in, 16)
            eng.dma_start(xin[:, :, :], x[:, 0:P, :].rearrange("b p d -> p b d")).then_inc(x_in, 16)
            eng.dma_start(wo32, wo.rearrange("(c p) n -> p c n", p=P)).then_inc(wo_in, 16)

            def load_bias(t, it, k):
                L, S, G = (t + 1) * P, bias_slots(t), len(groups(t))
                h = 4 * it + k
                if isinstance(it, int) and h < S:
                    if t > 0:
                        last = H - S + h if bias_slots(t - 1) == S else H - 1
                        eng.wait_ge(biased, group_at[t - 1] + len(groups(t - 1)) * B * (last + 1))
                else:
                    eng.wait_ge(biased, group_at[t] + G * B * (h - S + 1))
                eng.dma_start(bias_row(t, k, 0, L), bias[h, t * P:(t + 1) * P, 0:L]).then_inc(bias_in[k % S], 16)

            eng.wait_ge(weights_ready, 1)
            for t in range(QT):
                for k in range(2):
                    load_bias(t, 0, k)
                if t > 1:
                    eng.wait_ge(y_ready, B * (t - 1))
                    eng.dma_start(out[:, (t - 2) * P:(t - 1) * P, :].rearrange("b p d -> p b d"), y[:, :, :]
                                  ).then_inc(y_out, 16)
                if t + 1 < QT:
                    eng.wait_ge(unit_full, pro_base[t] + B)
                    eng.dma_start(xin[:, :, :], x[:, (t + 1) * P:(t + 2) * P, :].rearrange("b p d -> p b d")
                                  ).then_inc(x_in, 16)
                if t > 0:
                    eng.dma_start(xres[:, :, :], x[:, (t - 1) * P:t * P, :].rearrange("b p d -> p b d")
                                  ).then_inc(xres_in, 16)
                for k in range(2, 4):
                    load_bias(t, 0, k)
                with eng.Fori(1, TURNS) as it:
                    for k in range(4):
                        load_bias(t, it, k)
            for t in (QT - 1, QT):
                eng.wait_ge(y_ready, B * t)
                eng.dma_start(out[:, (t - 1) * P:t * P, :].rearrange("b p d -> p b d"), y[:, :, :]
                              ).then_inc(y_out, 16)
                if t < QT:
                    eng.dma_start(xres[:, :, :], x[:, t * P:(t + 1) * P, :].rearrange("b p d -> p b d")
                                  ).then_inc(xres_in, 16)
            eng.wait_ge(y_out, 16 * QT)

        @block.gpsimd
        def _(eng):
            links = [0]

            def link(ins):
                links[0] += 1
                ins.then_inc(pool_link, 1)
                eng.wait_ge(pool_link, links[0])

            nc.gpsimd.memset(powers[:, 0:1], 0.5)
            nc.gpsimd.memset(powers[:, 1:1 + B], -0.5)
            link(nc.gpsimd.memset(ident[:, :], 1.0))
            nc.gpsimd.affine_select(out=ident[:, :], in_=ident[:, :], pattern=[[-1, P]], compare_op=ALU.is_equal,
                                    fill=0.0, base=0, channel_multiplier=1).then_inc(ident_ready, 1)
            eng.wait_ge(maxes_ready, 1)
            nc.gpsimd.partition_all_reduce(allmax[:, :], maxes[:, :], P, ABSMAX).then_inc(allmax_ready, 1)

            far = eng.to_reg(-FAR)
            eng.wait_ge(square_ready, 1)
            nc.gpsimd.tensor_tensor(sc[:, 2:3], sc[:, 1:2], powers[:, 0:1], ALU.pow).then_inc(root_ready, 1)

            def inverse_std(a, eps):
                link(nc.gpsimd.tensor_scalar(a[:, :, 1], a[:, :, 1], eps, None, ALU.add))
                return nc.gpsimd.tensor_tensor(a[:, :, 1], a[:, :, 1], powers[:, 1:1 + B], ALU.pow)

            def x_std(t):
                eng.wait_ge(xvar_ready, t + 1)
                inverse_std(xst, EPS).then_inc(xstd_ready, 1)

            def edge(t, it, k):
                S = bias_slots(t)
                eng.wait_ge(bias_in[k % S], 16 * (bias_at[t][k % S] + 4 // S * it + k // S + 1))
                stand(eng, pool_passed)
                d = bias_row(t, k, t * P, (t + 1) * P)
                nc.gpsimd.affine_select(out=d, in_=d, pattern=[[-1, P]], compare_op=ALU.is_ge, fill=far, base=0,
                                        channel_multiplier=1).then_inc(bias_ready, 1)

            def null_starts(t, it):
                nc.gpsimd.tensor_copy(start[:, :].rearrange("p (h b) -> p b h", b=B),
                                      nsn[:, t % 3, :, span(4 * it, 4)]).then_inc(start_ready, 1)

            def keep_maxima(t, it):
                eng.wait_ge(biased, group_of(t, it, BODY * len(groups(t))))
                ck = len(groups(t)) - 1
                return nc.gpsimd.tensor_copy(negm[:, t % 2, :, span(4 * it, 4)],
                                             rowmin[:, :, ck].rearrange("p (h b) -> p b h", b=B))

            def denominators(t):
                r = t % 2
                nc.gpsimd.tensor_tensor(pn[:, :, :], negm[:, r, :, :], nsn[:, t % 3, :, :], ALU.subtract
                                        ).then_inc(null_shift, 1)
                eng.wait_ge(null_p, t + 1)
                link(nc.gpsimd.tensor_tensor(den[:, :, :], pn[:, :, :], rsum[:, r, 0, :, :], ALU.add))
                if exps(t) > 1:
                    link(nc.gpsimd.tensor_tensor(den[:, :, :], den[:, :, :], rsum[:, r, 1, :, :], ALU.add))
                nc.gpsimd.tensor_scalar(den[:, :, :], den[:, :, :], PSCALE, None, ALU.mult).then_inc(den_ready, 1)
                for b in range(B):
                    link(nc.gpsimd.tensor_tensor(nullv[:, :, :], pn[:, b, :].unsqueeze(2).broadcast_to([P, H, DH]),
                                                 nv[:, :].unsqueeze(1).broadcast_to([P, H, DH]), ALU.mult))
                    if b == 0:
                        eng.wait_ge(o_out, (t + 1) * STEPS // 4)
                    ins = nc.gpsimd.tensor_tensor(att[:, r, b, :, :], att[:, r, b, :, :], nullv[:, :, :], ALU.add)
                    if b + 1 < B:
                        link(ins)
                    else:
                        ins.then_inc(o_sum, 1)

            def rows_out(t):
                eng.wait_ge(yvar_ready, t + 1)
                inverse_std(yst, sc[:, 8:9]).then_inc(ystd_ready, 1)
                for b in range(B):
                    eng.wait_ge(unit_free, epi_base[t] + UE - B + b + 1)
                    link(nc.gpsimd.tensor_tensor(y[:, b, :], y[:, b, :], gout[:, :], ALU.mult))
                    if b == 0:
                        eng.wait_ge(xres_in, 16 * (t + 1))
                    nc.gpsimd.tensor_tensor(y[:, b, :], y[:, b, :], xres[:, b, :], ALU.add).then_inc(y_ready, 1)

            def first_bias(t):
                eng.wait_ge(unit_free, pro_base[t] + UP)
                null_starts(t, 0)
                for k in range(early_edges(t)):
                    edge(t, 0, k)

            x_std(0)
            first_bias(0)
            for t in range(QT):
                def first():
                    if t + 1 < QT:
                        x_std(t + 1)

                def turn(it):
                    for k in range(early_edges(t), 4):
                        edge(t, it, k)
                    if not isinstance(it, int) or it < TURNS - 1:
                        keep_maxima(t, it)
                        null_starts(t, it + 1)
                        for k in range(early_edges(t)):
                            edge(t, it + 1, k)
                    else:
                        link(keep_maxima(t, it))
                        if t + 1 < QT:
                            first_bias(t + 1)

                def between():
                    if t > 0:
                        denominators(t - 1)
                        rows_out(t - 1)

                tile_loop(eng, t, first, turn, between)
            denominators(QT - 1)
            rows_out(QT - 1)

        @block.tensor
        def _(eng):
            def unit(n):
                if not isinstance(n, int) or n >= TP:
                    eng.wait_ge(unit_free, n - TP + 1)

            def products(dst, pairs):
                for i, (a, m) in enumerate(pairs):
                    ins = nc.tensor.matmul(dst, a, m, start=i == 0, stop=i == len(pairs) - 1, skip_group_check=True)
                return ins

            def prologue(t):
                u0 = pro_base[t]
                for b in range(B):
                    unit(u0 + b)
                    eng.wait_ge(xn_ready, B * t + b + 1)
                    for c in range(C):
                        ins = nc.tensor.transpose(tp[:, (u0 + b) % TP, c * P:(c + 1) * P],
                                                  xin[:, b, c * P:(c + 1) * P], ident[:, :])
                    ins.then_inc(unit_full, 1)
                eng.wait_ge(unit_free, u0 + B)
                if t == 0:
                    eng.wait_ge(weights_ready, 1)
                for n in range(UQ):
                    unit(u0 + UX + n)
                    for m in range(2):
                        w = slice((2 * n + m) * P, (2 * n + m + 1) * P)
                        ins = products(tp[:, (u0 + UX + n) % TP, m * B * P:(m + 1) * B * P],
                                       [(wqs[:, c, w], xs[:, c, :, :].rearrange("p b q -> p (b q)"))
                                        for c in range(C) for wqs, xs in ((wqh, xth), (wqh, xtl), (wql, xth))])
                    ins.then_inc(unit_full, 1)
                un = u0 + UX + UQ
                unit(un)
                products(tp[:, un % TP, 0:B * P],
                         [(ws[:, c, :, :].rearrange("p a d -> p (a d)"), xs[:, c, :, :].rearrange("p b q -> p (b q)"))
                          for c in range(C) for ws, xs in ((wkh, xth), (wkh, xtl), (wkl, xth))]
                         ).then_inc(unit_full, 1)
                un += 1
                unit(un)
                for b in range(B):
                    ins = products(tp[:, un % TP, b * P:b * P + NSN],
                                   [(xs[:, c, b, :], ws[:, c, :])
                                    for c in range(C) for ws, xs in ((wvh, xth), (wvh, xtl), (wvl, xth))])
                ins.then_inc(unit_full, 1)

            def epilogue(t):
                u0 = epi_base[t]
                eng.wait_ge(att_ready, t + 1)
                un = u0
                for b in range(B):
                    rows = att[:, t % 2, b, :, :].rearrange("p h d -> p (h d)")
                    for c0 in range(0, CO, GROUP):
                        unit(un)
                        for c in range(c0, c0 + GROUP):
                            ins = nc.tensor.transpose(tp[:, un % TP, (c - c0) * P:(c - c0 + 1) * P],
                                                      rows[:, c * P:(c + 1) * P], ident[:, :])
                        ins.then_inc(unit_full, 1)
                        un += 1
                for b in range(B):
                    unit(un)
                    eng.wait_ge(unit_free, u0 + (b + 1) * (CO // GROUP))
                    products(tp[:, un % TP, 0:D],
                             [(a[:, b, c, :], w[:, c, :])
                              for c in range(CO) for a, w in ((ath, woh), (ath, wol), (atl, woh))]
                             ).then_inc(unit_full, 1)
                    un += 1

            def scores(t, it, f):
                it, f, j, ck = locate(t, it, f)
                h = 4 * it + j // 2
                a, e = chunk(t, ck)
                n = group_of(t, it, f)
                if not isinstance(n, int) or n > 1:
                    eng.wait_ge(biased, n - 1)
                dst = sp[:, f % 2, 0:e - a]
                nc.tensor.matmul(dst, qa[:, t % 2, h, j % 2, :], k1[:, j % 2, a:e], start=True, stop=False,
                                 skip_group_check=True)
                nc.tensor.matmul(dst, qb[0:DH + 1, t % 2, h, j % 2, :], k2[0:DH + 1, j % 2, a:e], start=False,
                                 stop=True, skip_group_check=True).then_inc(scores_full, 1)

            def turn_p(t, it, f):
                it, f, j, g = locate(t, it, f)
                unit(unit_of(t, it, f))
                if g % 2 == 0:
                    eng.wait_ge(exp_done, exp_at[t] + exps(t) * (BODY * it + j) + g // 2 + 1)
                for i, kb in enumerate(groups(t)[g]):
                    ins = nc.tensor.transpose(tp[:, slot_of(t, it, f), i * P:(i + 1) * P],
                                              ps[:, j % 4, kb * P:(kb + 1) * P], ident[:, :])
                ins.then_inc(unit_full, 1)

            def times_v(t, it, f):
                it, f, j, g = locate(t, it, f)
                eng.wait_ge(unit_free, unit_of(t, it, f) + 1)
                if g == 0 and j % 4 == 0:
                    n = t * (STEPS // 4) + 2 * it + j // 4
                    if not isinstance(n, int) or n > 1:
                        eng.wait_ge(o_out, n - 1)
                dst = op[:, j // 4, (j % 4) * DH:(j % 4 + 1) * DH]
                for i, kb in enumerate(groups(t)[g]):
                    a = slice(i * P, (i + 1) * P)
                    nc.tensor.matmul(dst, pth[:, f % 4, a], v[:, kb, j % 2, 0, :], start=kb == 0, stop=False,
                                     skip_group_check=True)
                    nc.tensor.matmul(dst, pth[:, f % 4, a], v[:, kb, j % 2, 1, :], start=False, stop=False,
                                     skip_group_check=True)
                    ins = nc.tensor.matmul(dst, ptl[:, f % 4, a], v[:, kb, j % 2, 0, :], start=False, stop=kb == t,
                                           skip_group_check=True)
                ins.then_inc(pv_done, 1)

            eng.wait_ge(ident_ready, 1)
            prologue(0)
            for t in range(QT):
                G = len(groups(t))
                if t == 0:
                    eng.wait_ge(qb_ready, 1)
                    eng.wait_ge(unit_free, pro_base[0] + UP)
                    for n in range(scored(0)):
                        scores(0, 0, n)

                def first():
                    for f in range(AHEAD):
                        turn_p(t, 0, f)
                        scores(t, 0, scored(t) + f)

                def next_scores(n):
                    if n == 0:
                        eng.wait_ge(qb_ready, t + 2)
                        eng.wait_ge(unit_free, pro_base[t + 1] + UP)
                    scores(t + 1, 0, n)

                def turn(it):
                    ahead = look_ahead(t, it, lambda it, f: scores(t, it, f), next_scores)
                    for f in range(BODY * G):
                        if here(it, f + AHEAD, t):
                            turn_p(t, it, f + AHEAD)
                        ahead(f)
                        times_v(t, it, f)

                def between():
                    if t + 1 < QT:
                        prologue(t + 1)
                    if t > 0:
                        epilogue(t - 1)

                tile_loop(eng, t, first, turn, between)
            epilogue(QT - 1)

        @block.scalar
        def _(eng):
            def small(dst, src):
                eng.dma_start(dst, src).then_inc(small_in, 16)

            small(gcol[:, :], g_in)
            small(nk[:, :], bc(cond[0], DH))
            small(nv[:, :], bc(cond[1], DH))
            small(nb[:, :], bc(null_bias, H))
            small(gout[:, :], bc(g_out, D))
            eng.dma_start(mask8[DH:DH + 1, :, :], mask.rearrange("(a b) n -> a b n", a=1)).then_inc(mask_in, 16)

            def high(dst, src, scale=1.0):
                return nc.scalar.activation(dst, src, ACT.Copy, scale=scale)

            def prologue(t):
                u0, n = pro_base[t], pro_base[t]
                for b in range(B):
                    eng.wait_ge(unit_full, n + 1)
                    high(xth[:, :, b, :], tp[:, n % TP, :].rearrange("p (c q) -> p c q", c=C)).then_inc(unit_high, 1)
                    n += 1
                for i in range(UQ):
                    eng.wait_ge(unit_full, n + 1)
                    for odd in range(2):
                        ins = high(qa[0:DH, t % 2, 4 * i + odd:4 * i + odd + 3:2, :, :],
                                   tp[DH * odd:DH * odd + DH, n % TP, :].rearrange("p (m b q) -> p m b q", m=2, b=B))
                    ins.then_inc(unit_high, 1)
                    n += 1
                eng.wait_ge(unit_full, n + 1)
                high(k1[:, :, t * P:(t + 1) * P], tp[:, n % TP, 0:B * P].rearrange("p (b q) -> p b q", b=B)
                     ).then_inc(unit_high, 1)
                n += 1
                eng.wait_ge(unit_full, n + 1)
                high(v[:, t, :, 0, :], tp[:, n % TP, 0:B * P].rearrange("p (b q) -> p b q", b=B)[:, :, 0:DH]
                     ).then_inc(unit_high, 1)

            def null_weights(t):
                eng.wait_ge(null_shift, t + 1)
                nc.scalar.activation(pn[:, :, :], pn[:, :, :], ACT.Exp).then_inc(null_p, 1)

            def epilogue(t):
                n = epi_base[t]
                for b in range(B):
                    for c0 in range(0, CO, GROUP):
                        eng.wait_ge(unit_full, n + 1)
                        high(ath[:, b, c0:c0 + GROUP, :], tp[:, n % TP, :].rearrange("p (c q) -> p c q", c=GROUP)
                             ).then_inc(unit_high, 1)
                        n += 1

            def exp(t, it, j, c):
                it, j = it + j // BODY, j % BODY
                G, h = len(groups(t)), 4 * it + j // 2
                if c == 0:
                    eng.wait_ge(biased, group_of(t, it, G * (j + 1)))
                a, e = chunk(t, c, EXP)
                nc.scalar.activation(ps[:, j % 4, a:e], ps[:, j % 4, a:e], ACT.Exp, bias=rowmin[:, j, G - 1:G],
                                     scale=-1.0, accum_out=rsum[:, t % 2, c, j % 2, span(h, 1)]
                                     ).then_inc(exp_done, 1)

            def p_high(t, it, f):
                it, f, j, g = locate(t, it, f)
                eng.wait_ge(unit_full, unit_of(t, it, f) + 1)
                n = group_of(t, it, f)
                if not isinstance(n, int) or n > 3:
                    eng.wait_ge(pv_done, n - 3)
                w = len(groups(t)[g]) * P
                high(pth[:, f % 4, 0:w], tp[:, slot_of(t, it, f), 0:w], PSCALE).then_inc(unit_high, 1)

            def take_o(t, it, j):
                eng.wait_ge(pv_done, group_of(t, it, len(groups(t)) * (j + 1)))
                h = 4 * it + 2 * (j // 4)
                for b in range(B):
                    ins = high(att[:, t % 2, b, span(h, 2), :],
                               op[:, j // 4, 0:4 * DH].rearrange("p (h b d) -> p h b d", h=2, b=B)[:, :, b, :])
                ins.then_inc(o_out, 1)

            def first_exps(t):
                for j in range(lead(t)):
                    for c in range(exps(t)):
                        exp(t, 0, j, c)

            def next_exps(t):
                G = len(groups(t))
                own = (BODY - lead(t)) * G - 1 - AHEAD
                with_bias = BODY * G - AHEAD - scored(t) + lead(t + 1) * len(groups(t + 1))
                return min(max(own, with_bias), BODY * G - 1)

            prologue(0)
            for t in range(QT):
                G = len(groups(t))
                if t == 0:
                    first_exps(0)

                def group(it, f):
                    p_high(t, it, f)
                    it, f, j, g = locate(t, it, f)
                    if g % 2 == 0 and here(it, f + lead(t) * G, t):
                        exp(t, it, j + lead(t), g // 2)

                def first():
                    for f in range(AHEAD):
                        group(0, f)

                def turn(it):
                    last = isinstance(it, int) and it == TURNS - 1
                    for f in range(BODY * G):
                        if here(it, f + AHEAD, t):
                            group(it, f + AHEAD)
                        if last and t + 1 < QT and f == next_exps(t):
                            first_exps(t + 1)
                        if f == 4 * G + 1:
                            take_o(t, it, 3)
                    take_o(t, it, 7)

                def between():
                    if t > 0:
                        null_weights(t - 1)
                    if t + 1 < QT:
                        prologue(t + 1)
                    if t > 0:
                        epilogue(t - 1)

                tile_loop(eng, t, first, turn, between)
            null_weights(QT - 1)
            epilogue(QT - 1)

        @block.vector
        def _(eng):
            links = [0]

            def link(ins):
                links[0] += 1
                ins.then_inc(dve_link, 1)
                eng.wait_ge(dve_link, links[0])

            def low(dst, src, hi_half, scale=1.0):
                return nc.vector.scalar_tensor_tensor(out=dst, in0=src, scalar=scale, in1=hi_half, op0=ALU.mult,
                                                      op1=ALU.subtract)

            def setup():
                nc.vector.memset(maxes[:, :], 0.0)
                nc.vector.memset(rowmin[:, :, :], 0.0)
                eng.wait_ge(small_in, 16 * 5)
                eng.wait_ge(wkv_in, 16)
                for c in range(C):
                    nc.vector.tensor_scalar(wkv32[:, c, :], wkv32[:, c, :], gcol[:, c:c + 1], None, ALU.mult)
                eng.wait_ge(wq_in, 16)
                for c in range(C):
                    ins = nc.vector.tensor_scalar(wq32[:, c, :], wq32[:, c, :], gcol[:, c:c + 1], None, ALU.mult)
                link(ins)
                for c in range(C):
                    ins = nc.vector.scalar_tensor_tensor(
                        out=tmp[:, c, :].rearrange("p (h d) -> p h d", d=DH),
                        in0=wq32[:, c, :].rearrange("p (h d) -> p h d", d=DH), scalar=DH ** -0.5,
                        in1=nk[:, :].unsqueeze(1).broadcast_to([P, H, DH]), op0=ALU.mult, op1=ALU.mult)
                link(ins)
                for c in range(C):
                    ins = nc.vector.tensor_reduce(wn32[:, c, :], tmp[:, c, :].rearrange("p (h d) -> p h d", d=DH),
                                                  AX_X, ALU.add)
                link(ins)

                def largest(k, a):
                    nc.vector.tensor_reduce(maxes[:, k:k + 1], a, mybir.AxisListType.XY, ALU.max)
                    return nc.vector.tensor_reduce(maxes[:, 6 + k:7 + k], a, mybir.AxisListType.XY, ALU.min)

                largest(0, wq32)
                largest(1, wkv32[:, :, 0:DH])
                largest(2, wkv32[:, :, DH:2 * DH])
                largest(3, wn32)
                eng.wait_ge(wo_in, 16)
                largest(4, wo32)
                largest(5, nv[:, :].unsqueeze(1)).then_inc(maxes_ready, 1)
                eng.wait_ge(allmax_ready, 1)

                def col(k):
                    return sc[:, k:k + 1]

                link(nc.vector.scalar_tensor_tensor(out=allmax[:, 0:6], in0=allmax[:, 0:6], scalar=1e-18,
                                                    in1=allmax[:, 6:12], op0=ALU.max, op1=ALU.max))
                aq, ak, av, an, aw, anv = (allmax[:, k:k + 1] for k in range(6))
                link(nc.vector.reciprocal(col(0), ak))
                nc.vector.tensor_scalar(col(1), col(0), aq, DH ** -0.5, ALU.mult, ALU.mult).then_inc(square_ready, 1)
                eng.wait_ge(root_ready, 1)
                link(nc.vector.reciprocal(col(3), col(2)))
                nc.vector.tensor_scalar(col(3), col(3), DH ** -0.5, None, ALU.mult)
                link(nc.vector.tensor_scalar(col(4), anv, 1.0 / D, av, ALU.mult, ALU.max))
                link(nc.vector.reciprocal(col(4), col(4)))
                nc.vector.tensor_scalar(col(4), col(4), 16.0, None, ALU.mult)
                link(nc.vector.reciprocal(col(5), an))
                nc.vector.tensor_scalar(col(5), col(5), 16.0, None, ALU.mult)
                nc.vector.tensor_scalar(col(6), an, -1.0 / 16.0, None, ALU.mult)
                link(nc.vector.reciprocal(col(7), aw))
                link(nc.vector.tensor_scalar(col(7), col(7), 1024.0, None, ALU.mult))
                link(nc.vector.tensor_scalar(col(8), col(4), col(7), None, ALU.mult))
                link(nc.vector.tensor_scalar(col(8), col(8), col(8), EPS, ALU.mult, ALU.mult))
                nc.vector.tensor_scalar(nv[:, :], nv[:, :], col(4), PSCALE, ALU.mult, ALU.mult)
                nc.vector.tensor_scalar(wq32, wq32, col(3), None, ALU.mult)
                nc.vector.tensor_scalar(wo32, wo32, col(7), None, ALU.mult)
                nc.vector.tensor_scalar(wkv32[:, :, 0:DH], wkv32[:, :, 0:DH], col(2), None, ALU.mult)
                nc.vector.tensor_scalar(wkv32[:, :, DH:2 * DH], wkv32[:, :, DH:2 * DH], col(4), None, ALU.mult)
                link(nc.vector.tensor_scalar(wn32, wn32, col(5), None, ALU.mult))
                nc.vector.tensor_copy(wqh[:, :, :], wq32)
                nc.vector.tensor_copy(woh[:, :, :], wo32)
                for a in range(2):
                    nc.vector.tensor_copy(wkh[:, :, a, :], wkv32[:, :, 0:DH])
                nc.vector.tensor_copy(wvh[:, :, 0:DH], wkv32[:, :, DH:2 * DH])
                link(nc.vector.tensor_copy(wvh[:, :, DH:NSN], wn32))
                nc.vector.tensor_tensor(wql[:, :, :], wq32, wqh[:, :, :], ALU.subtract)
                nc.vector.tensor_tensor(wol[:, :, :], wo32, woh[:, :, :], ALU.subtract)
                for a in range(2):
                    nc.vector.tensor_tensor(wkl[:, :, a, :], wkv32[:, :, 0:DH], wkh[:, :, a, :], ALU.subtract)
                nc.vector.tensor_tensor(wvl[:, :, 0:DH], wkv32[:, :, DH:2 * DH], wvh[:, :, 0:DH], ALU.subtract)
                nc.vector.tensor_tensor(wvl[:, :, DH:NSN], wn32, wvh[:, :, DH:NSN], ALU.subtract)
                nc.vector.memset(qb[DH:DH + 1, :, :, :, :], MASK_ONE)
                eng.wait_ge(mask_in, 16)
                nc.vector.tensor_scalar(k2[DH:DH + 1, :, :], mask8[DH:DH + 1, :, :], -1.0, MASK_FAR, ALU.add,
                                        ALU.mult).then_inc(weights_ready, 1)

            def moments(dst, b, src):
                link(nc.vector.bn_stats(st[:, b, 0:6], src))
                return nc.vector.bn_aggr(dst[:, b, :], st[:, b, 0:6])

            def moments_x(t):
                eng.wait_ge(x_in, 16 * (t + 1))
                for b in range(B):
                    ins = moments(xst, b, xin[:, b, :])
                ins.then_inc(xvar_ready, 1)

            def norm_x(t):
                eng.wait_ge(xstd_ready, t + 1)
                for b in range(B):
                    nc.vector.tensor_scalar(xin[:, b, :], xin[:, b, :], xst[:, b, 0:1], xst[:, b, 1:2], ALU.subtract,
                                            ALU.mult).then_inc(xn_ready, 1)

            def prologue(t):
                n, h = pro_base[t], pro_high[t]
                for b in range(B):
                    eng.wait_ge(unit_high, h + 1)
                    low(xtl[:, :, b, :], tp[:, n % TP, :].rearrange("p (c q) -> p c q", c=C), xth[:, :, b, :]
                        ).then_inc(unit_free, 1)
                    n, h = n + 1, h + 1
                for i in range(UQ):
                    eng.wait_ge(unit_high, h + 1)
                    for odd in range(2):
                        hs = slice(4 * i + odd, 4 * i + odd + 3, 2)
                        ins = low(qa[DH:P, t % 2, hs, :, :],
                                  tp[DH * odd:DH * odd + DH, n % TP, :].rearrange("p (m b q) -> p m b q", m=2, b=B),
                                  qa[0:DH, t % 2, hs, :, :])
                    ins.then_inc(unit_free, 1)
                    n, h = n + 1, h + 1
                nc.vector.tensor_copy(qb[0:DH, t % 2, :, :, :], qa[0:DH, t % 2, :, :, :]).then_inc(qb_ready, 1)
                eng.wait_ge(unit_high, h + 1)
                low(k2[0:DH, :, t * P:(t + 1) * P], tp[0:DH, n % TP, 0:B * P].rearrange("p (b q) -> p b q", b=B),
                    k1[0:DH, :, t * P:(t + 1) * P]).then_inc(unit_free, 1)
                n, h = n + 1, h + 1
                eng.wait_ge(unit_high, h + 1)
                vals = tp[:, n % TP, 0:B * P].rearrange("p (b q) -> p b q", b=B)
                low(v[:, t, :, 1, :], vals[:, :, 0:DH], v[:, t, :, 0, :])
                nc.vector.scalar_tensor_tensor(
                    out=nsn[:, t % 3, :, :], in0=vals[:, :, DH:NSN], scalar=sc[:, 6:7],
                    in1=nb[:, :].unsqueeze(1).broadcast_to([P, B, H]), op0=ALU.mult, op1=ALU.subtract
                ).then_inc(unit_free, 1)

            def epilogue(t):
                eng.wait_ge(den_ready, t + 1)
                link(nc.vector.reciprocal(den[:, :, :], den[:, :, :]))
                eng.wait_ge(o_sum, t + 1)
                nc.vector.tensor_tensor(att[:, t % 2, :, :, :], att[:, t % 2, :, :, :],
                                        den[:, :, :].unsqueeze(3).broadcast_to([P, B, H, DH]), ALU.mult
                                        ).then_inc(att_ready, 1)
                n, h = epi_base[t], epi_high[t]
                for b in range(B):
                    for c0 in range(0, CO, GROUP):
                        eng.wait_ge(unit_high, h + 1)
                        low(atl[:, b, c0:c0 + GROUP, :], tp[:, n % TP, :].rearrange("p (c q) -> p c q", c=GROUP),
                            ath[:, b, c0:c0 + GROUP, :]).then_inc(unit_free, 1)
                        n, h = n + 1, h + 1
                if t > 0:
                    eng.wait_ge(y_out, 16 * t)
                for b in range(B):
                    eng.wait_ge(unit_full, n + b + 1)
                    ins = moments(yst, b, tp[:, (n + b) % TP, 0:D])
                ins.then_inc(yvar_ready, 1)
                eng.wait_ge(ystd_ready, t + 1)
                for b in range(B):
                    nc.vector.tensor_scalar(y[:, b, :], tp[:, (n + b) % TP, 0:D], yst[:, b, 0:1], yst[:, b, 1:2],
                                            ALU.subtract, ALU.mult).then_inc(unit_free, 1)

            def add_bias(t, it, f):
                it, f, j, ck = locate(t, it, f)
                n = group_of(t, it, f)
                eng.wait_ge(scores_full, n + 1)
                if ck == 0:
                    if j % 2 == 0:
                        eng.wait_ge(bias_ready, H * t + 4 * it + j // 2 + 1)
                    if j == 0:
                        eng.wait_ge(start_ready, TURNS * t + it + 1)
                    least = start[:, j:j + 1]
                else:
                    eng.wait_ge(biased, n)
                    least = rowmin[:, j, ck - 1:ck]
                stand(eng, dve_passed)
                a, e = chunk(t, ck)
                nc.vector.tensor_tensor_reduce(ps[:, j % 4, a:e], sp[:, f % 2, 0:e - a], bias_row(t, j // 2, a, e),
                                               -1.0, least, ALU.add, ALU.min, rowmin[:, j, ck:ck + 1]
                                               ).then_inc(biased, 1)

            def p_low(t, it, f):
                it, f, j, g = locate(t, it, f)
                eng.wait_ge(unit_high, high_of(t, it, f) + 1)
                w = len(groups(t)[g]) * P
                low(ptl[:, f % 4, 0:w], tp[:, slot_of(t, it, f), 0:w], pth[:, f % 4, 0:w], PSCALE
                    ).then_inc(unit_free, 1)

            setup()
            moments_x(0)
            norm_x(0)
            prologue(0)
            for t in range(QT):
                G = len(groups(t))
                if t == 0:
                    for n in range(scored(0)):
                        add_bias(0, 0, n)

                def first():
                    if t + 1 < QT:
                        moments_x(t + 1)
                    for f in range(AHEAD):
                        p_low(t, 0, f)
                        add_bias(t, 0, scored(t) + f)
                    if t + 1 < QT:
                        norm_x(t + 1)

                def turn(it):
                    ahead = look_ahead(t, it, lambda it, f: add_bias(t, it, f), lambda n: add_bias(t + 1, 0, n))
                    for f in range(BODY * G):
                        if here(it, f + AHEAD, t):
                            p_low(t, it, f + AHEAD)
                        ahead(f)

                def between():
                    if t + 1 < QT:
                        prologue(t + 1)
                    if t > 0:
                        epilogue(t - 1)

                tile_loop(eng, t, first, turn, between)
            epilogue(QT - 1)


_INS = ['x', 'fside_16xSxS_0', 'cond_64', 'mask_BxS_bk0', 'L0_cond_g_in', 'L0_cond_null_attn_bias', 'L0_cond_Wq',
        'L0_cond_Wkv', 'L0_cond_Wo', 'L0_cond_g_out']


def kernel(**inputs):
    import numpy as np
    import concourse.bacc as bacc
    from concourse.bass_utils import run_bass_kernel_spmd

    nc = bacc.Bacc("TRN2", target_bir_lowering=False, num_devices=1)
    arrays, args = {}, []
    for name in _INS:
        a = np.ascontiguousarray(inputs[name])
        if name == 'L0_cond_g_in':
            a = np.ascontiguousarray(a.reshape(-1, P).T)
        arrays[f"in_{name}"] = a
        args.append(nc.dram_tensor(f"in_{name}", a.shape, mybir.dt.from_np(a.dtype), kind="ExternalInput").ap())
    out = nc.dram_tensor("out", arrays["in_x"].shape, F32, kind="ExternalOutput").ap()
    cond_attention(nc, *args, out)
    r = run_bass_kernel_spmd(nc, [arrays], core_ids=[0])
    return r.results[0]["out"]
```

```python
from contextlib import ExitStack

import concourse.bass as bass
from concourse import mybir

F32 = mybir.dt.float32
F16 = mybir.dt.float16
ALU = mybir.AluOpType
ACT = mybir.ActivationFunctionType
AX_X = mybir.AxisListType.X
ABSMAX = bass.bass_isa.ReduceOp.absmax

P = 128
DH = 64
GROUP = 4
CHUNK = GROUP * P
EXP = 2 * CHUNK
AHEAD = 3
SCORES_AHEAD = 2
TP = 4
BODY = 8
PEELED = 2
EPS = 1e-5
FAR = 1e30
PSCALE = 16384.0
MASK_ONE, MASK_FAR = 32768.0, 60000.0


def cond_attention(nc, x, bias, cond, mask, g_in, null_bias, wq, wkv, wo, g_out, out):
    B, N, D = x.shape
    H = bias.shape[0]
    INNER = H * DH
    QT = N // P
    C = D // P
    CO = INNER // P
    STEPS = H * B
    TURNS = STEPS // BODY
    NSN = DH + H
    assert B == 2 and D == C * P and BODY == 4 * B and STEPS % BODY == 0

    with ExitStack() as ctx:
        def sb(name, shape, dt):
            return ctx.enter_context(nc.sbuf_tensor(name, shape, dt))

        def sem(name):
            return ctx.enter_context(nc.semaphore(name))

        ident = sb("ident", [P, P], F32)
        wqh = sb("wqh", [P, C, INNER], F16)
        wql = sb("wql", [P, C, INNER], F16)
        wkh = sb("wkh", [P, C, 2, DH], F16)
        wkl = sb("wkl", [P, C, 2, DH], F16)
        wvh = sb("wvh", [P, C, NSN], F16)
        wvl = sb("wvl", [P, C, NSN], F16)
        woh = sb("woh", [P, CO, D], F16)
        wol = sb("wol", [P, CO, D], F16)
        gcol = sb("gcol", [P, C], F32)
        gout = sb("gout", [P, D], F32)
        nv = sb("nv", [P, DH], F32)
        nb = sb("nb", [P, H], F32)
        maxes = sb("maxes", [P, 24], F32)
        allmax = sb("allmax", [P, 24], F32)
        gq = sb("gq", [P, C], F32)
        sc = sb("sc", [P, 16], F32)
        powers = sb("powers", [P, 4], F32)
        k1 = sb("k1", [P, B, N], F16)
        k2 = sb("k2", [P, B, N], F16)
        v = sb("v", [P, QT, B, 2, DH], F16)
        xin = sb("xin", [P, B, D], F32)
        xres = sb("xres", [P, B, D], F32)
        xth = sb("xth", [P, C, B, P], F16)
        xtl = sb("xtl", [P, C, B, P], F16)
        qa = sb("qa", [P, 2, H, B, P], F16)
        qb = sb("qb", [P, 2, H, B, P], F16)
        st = sb("st", [P, B, 8], F32)
        yhalf = sb("yhalf", [P, B, 2, 6], F32)
        xst = sb("xst", [P, B, 2], F32)
        yst = sb("yst", [P, B, 2], F32)
        bs = sb("bs", [P, 2 * N], F32)
        ps = sb("ps", [P, 4, N], F32)
        pth = sb("pth", [P, 4, GROUP * P], F16)
        ptl = sb("ptl", [P, 4, GROUP * P], F16)
        rowmin = sb("rowmin", [P, BODY, 4], F32)
        start = sb("start", [P, BODY], F32)
        nsn = sb("nsn", [P, 3, B, H], F32)
        rsum = sb("rsum", [P, 2, 2, B, H], F32)
        pn = sb("pn", [P, B, H], F32)
        den = sb("den", [P, B, 4], F32)
        att = sb("att", [P, 2, B, H, DH], F32)
        nullv = sb("nullv", [P, B, 4, DH], F32)
        ath = sb("ath", [P, B, CO, P], F16)
        atl = sb("atl", [P, B, CO, P], F16)
        y = sb("y", [P, B, D], F32)
        rows_of = [y] * (QT - 1) + [xin]

        W0 = N // 2
        assert P * (QT // 2) == W0 and 4 * (N - W0) == CO * D
        wq32 = bs[:, :].rearrange("p (c n) -> p c n", n=INNER)
        tmp = att[:, :, :, :, :].rearrange("p a b h d -> p (a b h d)").rearrange("p (c n) -> p c n", n=INNER)
        wo32 = ps[:, :, W0:N]
        wkv32 = ps[:, 2, W0 - C * 2 * DH:W0].rearrange("p (c n) -> p c n", c=C)
        wn32 = ps[:, 3, W0 - C * H:W0].rearrange("p (c h) -> p c h", c=C)
        nk = ps[:, 3, W0 - C * H - DH:W0 - C * H]
        mask8 = y[:, :, :].rearrange("p b d -> p (b d)").bitcast(mybir.dt.uint8).rearrange("p (b n) -> p b n", b=B)

        sp = ctx.enter_context(nc.psum_tensor("sp", [P, 2, CHUNK], F32))
        tp = ctx.enter_context(nc.psum_tensor("tp", [P, TP, 512], F32))
        op = ctx.enter_context(nc.psum_tensor("op", [P, 2, 512], F32))

        wkv_in, wo_in = sem("wkv_in"), sem("wo_in")
        wq_in = [sem(f"wq_in{c}") for c in range(C)]
        small_in, mask_in = sem("small_in"), sem("mask_in")
        x_in, xres_in = sem("x_in"), sem("xres_in")
        bias_in = [sem(f"bias_in{k}") for k in range(4)]
        y_out = sem("y_out")
        ident_ready = sem("ident_ready")
        maxes_ready = sem("maxes_ready")
        allmax_ready = sem("allmax_ready")
        square_ready = sem("square_ready")
        root_ready = sem("root_ready")
        xvar_ready = sem("xvar_ready")
        product_ready = sem("product_ready")
        scales_ready = sem("scales_ready")
        whigh_ready = sem("whigh_ready")
        weights_ready = sem("weights_ready")
        wo_ready = sem("wo_ready")
        dve_passed = sem("dve_passed")
        pool_passed = sem("pool_passed")
        dve_link = sem("dve_link")
        pool_link = sem("pool_link")
        xstd_ready = sem("xstd_ready")
        xn_ready = sem("xn_ready")
        ystd_ready = sem("ystd_ready")
        yn_ready = sem("yn_ready")
        qb_in = sem("qb_in")
        unit_full = sem("unit_full")
        unit_high = sem("unit_high")
        unit_free = sem("unit_free")
        scores_full = sem("scores_full")
        biased = sem("biased")
        bias_ready = sem("bias_ready")
        start_ready = sem("start_ready")
        exp_done = sem("exp_done")
        pv_done = sem("pv_done")
        o_out = sem("o_out")
        null_shift = sem("null_shift")
        null_p = sem("null_p")
        den_ready = sem("den_ready")
        normal_step = sem("normal_step")
        inverse_ready = sem("inverse_ready")
        att_ready = sem("att_ready")
        y_ready = sem("y_ready")
        def stand(eng, passed):
            eng.sem_inc(passed, 1)

        def bc(row, n):
            return row.rearrange("(a n) -> a n", a=1).broadcast_to([P, n])

        def span(i, n):
            return slice(i, i + n) if isinstance(i, int) else bass.ds(i, n)

        def blocks(t):
            return t + 1

        def groups(t):
            return [range(g, min(g + GROUP, t + 1)) for g in range(0, t + 1, GROUP)]

        def chunk(t, ck, width=CHUNK):
            return ck * width, min((ck + 1) * width, (t + 1) * P)

        def exps(t):
            return -(-(t + 1) * P // EXP)

        def lead(t):
            return 2 if len(groups(t)) == 1 else 1

        def scored(t):
            G = len(groups(t))
            return min(2 * G + SCORES_AHEAD, 3 * G + 1)

        def bias_slots(t):
            return 4 if 4 * (t + 1) * P <= 2 * N else 2

        def early_edges(t):
            return -(-(AHEAD + scored(t)) // (B * len(groups(t))))

        def bias_row(t, h, a, e):
            at = (h % bias_slots(t)) * (2 * N // bias_slots(t))
            return bs[:, at + a:at + e]

        BESIDE = [("x", 0), ("x", 1), ("att", 0), ("att", 1), ("q", 0), ("q", 1), ("att", 2), ("q", 2), ("att", 3),
                  ("q", 3), ("out", 0), ("q", 4), ("q", 5), ("out", 1), ("q", 6), ("q", 7), ("out", 2), ("k", 0),
                  ("v", 0), ("out", 3)]
        PROLOGUE = [u for u in BESIDE if u[0] in "xqkv"]
        EPILOGUE = [u for u in BESIDE if u not in PROLOGUE]
        UQ = H // 2
        assert (B, H, CO, D) == (2, 16, 8, 512)

        number = {(0, *u): n for n, u in enumerate(PROLOGUE)}
        base, beside, group_at, exp_at, bias_at = {}, {}, {}, {}, {}
        u, ngroup, nexp = len(PROLOGUE), 0, 0
        uses = [0] * 4
        for t in range(QT):
            G = len(groups(t))
            base[t], beside[t] = u, []
            theirs = ([(t + 1, *e) for e in PROLOGUE] if t + 1 < QT else []) + (
                [(t - 1, *e) for e in EPILOGUE] if t > 0 else [])
            theirs.sort(key=lambda e: BESIDE.index(e[1:]))
            start_at, end_at = (TURNS - PEELED) * BODY * G, STEPS * G - AHEAD - scored(t) - 1
            for i, e in enumerate(theirs):
                at = start_at + i * (end_at - start_at) // len(theirs)
                beside[t].append((at, e))
                number[e] = u + at + AHEAD + 1 + i
            u += STEPS * G + len(theirs)
            group_at[t], exp_at[t], bias_at[t] = ngroup, nexp, list(uses)
            ngroup += STEPS * G
            nexp += STEPS * exps(t)
            for k in range(bias_slots(t)):
                uses[k] += H // bias_slots(t)
        for n, e in enumerate(EPILOGUE):
            number[(QT - 1, *e)] = u + n

        def units_beside(t, it, f):
            x = BODY * len(groups(t)) * it + f if isinstance(it, int) else None
            return [e for at, e in beside[t] if at == x]

        def locate(t, it, f):
            G = len(groups(t))
            it, f = it + f // (BODY * G), f % (BODY * G)
            return it, f, f // G, f % G

        def here(it, f, t):
            return not isinstance(it, int) or locate(t, it, f)[0] < TURNS

        def others(t, it, f):
            if not isinstance(it, int):
                return 0
            return sum(at + AHEAD < BODY * len(groups(t)) * it + f for at, _ in beside[t])

        def unit_of(t, it, f):
            return BODY * len(groups(t)) * it + f + base[t] + others(t, it, f)

        def slot_of(t, it, f):
            return (f + base[t] + others(t, it, f)) % TP

        def group_of(t, it, f):
            return group_at[t] + BODY * len(groups(t)) * it + f

        def tile_loop(eng, t, first, turn):
            first()
            if t == 0:
                turn(0)
            with eng.Fori(int(t == 0), TURNS - PEELED) as it:
                turn(it)
            for it in range(TURNS - PEELED, TURNS):
                turn(it)

        def look_ahead(t, it, take, take_next):
            G = len(groups(t))
            ahead = AHEAD + scored(t)

            def at(f):
                if here(it, f + ahead, t):
                    take(*locate(t, it, f + ahead)[0:2])
                elif t + 1 < QT:
                    n = f + ahead - BODY * G
                    todo = scored(t + 1)
                    if n < todo:
                        take_next(n)
                    if f == BODY * G - 1:
                        for m in range(n + 1, todo):
                            take_next(m)
            return at

        block = ctx.enter_context(nc.Block())

        @block.sync
        def _(eng):
            eng.dma_start(xin[:, :, :], x[:, 0:P, :].rearrange("b p d -> p b d")).then_inc(x_in, 16)
            eng.dma_start(wkv32, wkv.rearrange("(c p) n -> p c n", p=P)).then_inc(wkv_in, 16)
            for c in range(C):
                eng.dma_start(wq32[:, c, :], wq[c * P:(c + 1) * P, :]).then_inc(wq_in[c], 16)
            for k in range(4):
                eng.dma_start(wo32[:, k, :].rearrange("p (c n) -> p c n", n=D),
                              wo[2 * k * P:2 * (k + 1) * P, :].rearrange("(c p) n -> p c n", p=P)).then_inc(wo_in, 16)

            def load_bias(t, it, k):
                L, S, G = (t + 1) * P, bias_slots(t), len(groups(t))
                h = 4 * it + k
                if isinstance(it, int) and h < S:
                    if t > 0:
                        last = H - S + h if bias_slots(t - 1) == S else H - 1
                        eng.wait_ge(biased, group_at[t - 1] + len(groups(t - 1)) * B * (last + 1))
                else:
                    eng.wait_ge(biased, group_at[t] + G * B * (h - S + 1))
                eng.dma_start(bias_row(t, k, 0, L), bias[h, t * P:(t + 1) * P, 0:L]).then_inc(bias_in[k % S], 16)

            def store(t):
                eng.dma_start(out[:, t * P:(t + 1) * P, :].rearrange("b p d -> p b d"), rows_of[t][:, :, :]
                              ).then_inc(y_out, 16)

            def load_residual(t):
                eng.dma_start(xres[:, :, :], x[:, t * P:(t + 1) * P, :].rearrange("b p d -> p b d")
                              ).then_inc(xres_in, 16)

            eng.wait_ge(weights_ready, 1)
            eng.wait_ge(product_ready, C)
            for t in range(QT):
                for k in range(2):
                    load_bias(t, 0, k)
                if t + 1 < QT:
                    eng.wait_ge(unit_full, number[t, "x", B - 1] + 1)
                    eng.dma_start(xin[:, :, :], x[:, (t + 1) * P:(t + 2) * P, :].rearrange("b p d -> p b d")
                                  ).then_inc(x_in, 16)
                for k in range(2, 4):
                    load_bias(t, 0, k)
                with eng.Fori(1, TURNS - 1) as it:
                    for k in range(4):
                        load_bias(t, it, k)
                for k in range(bias_slots(t)):
                    load_bias(t, TURNS - 1, k)
                if t > 1:
                    eng.wait_ge(y_ready, B * (t - 1))
                    store(t - 2)
                if t > 0:
                    load_residual(t - 1)
                for k in range(bias_slots(t), 4):
                    load_bias(t, TURNS - 1, k)
            eng.wait_ge(y_ready, B * (QT - 1))
            store(QT - 2)
            load_residual(QT - 1)
            eng.wait_ge(y_ready, B * QT)
            store(QT - 1)
            eng.wait_ge(y_out, 16 * QT)

        @block.gpsimd
        def _(eng):
            links = [0]

            def link(ins):
                links[0] += 1
                ins.then_inc(pool_link, 1)
                eng.wait_ge(pool_link, links[0])

            nc.gpsimd.memset(powers[:, 0:1], 0.5)
            nc.gpsimd.memset(powers[:, 1:1 + B], -0.5)
            link(nc.gpsimd.memset(ident[:, :], 1.0))
            nc.gpsimd.affine_select(out=ident[:, :], in_=ident[:, :], pattern=[[-1, P]], compare_op=ALU.is_equal,
                                    fill=0.0, base=0, channel_multiplier=1).then_inc(ident_ready, 1)
            eng.wait_ge(ident_ready, 1)
            link(nc.gpsimd.memset(qb[DH:DH + 1, :, :, :, :], MASK_ONE))
            def inverse_std(a, eps):
                link(nc.gpsimd.tensor_scalar(a[:, :, 1], a[:, :, 1], eps, None, ALU.add))
                return nc.gpsimd.tensor_tensor(a[:, :, 1], a[:, :, 1], powers[:, 1:1 + a.shape[1]], ALU.pow)

            def x_std(t):
                eng.wait_ge(xvar_ready, t + 1)
                inverse_std(xst, EPS).then_inc(xstd_ready, 1)

            def y_std(t, b=B - 1):
                eng.wait_ge(unit_free, number[t, "out", 2 * b + 1] + 1)
                inverse_std(yst if t < QT - 1 else yst[:, b:b + 1, :], sc[:, 8:9]).then_inc(ystd_ready, 1)

            def edge(t, it, k):
                S = bias_slots(t)
                eng.wait_ge(bias_in[k % S], 16 * (bias_at[t][k % S] + 4 // S * it + k // S + 1))
                stand(eng, pool_passed)
                d = bias_row(t, k, t * P, (t + 1) * P)
                nc.gpsimd.affine_select(out=d, in_=d, pattern=[[-1, P]], compare_op=ALU.is_ge, fill=far, base=0,
                                        channel_multiplier=1).then_inc(bias_ready, 1)

            def null_starts(t, it):
                nc.gpsimd.tensor_copy(start[:, :].rearrange("p (h b) -> p b h", b=B),
                                      nsn[:, t % 3, :, span(4 * it, 4)]).then_inc(start_ready, 1)

            def null_shifts(t, it):
                eng.wait_ge(biased, group_of(t, it, BODY * len(groups(t))))
                stand(eng, pool_passed)
                ck = len(groups(t)) - 1
                nc.gpsimd.tensor_tensor(pn[:, :, span(4 * it, 4)], rowmin[:, :, ck].rearrange("p (h b) -> p b h", b=B),
                                        nsn[:, t % 3, :, span(4 * it, 4)], ALU.subtract).then_inc(null_shift, 1)

            def normalise(t, it):
                r, heads = t % 2, span(4 * it, 4)
                parts = exps(t)
                done = sum((2 + exps(e)) * TURNS for e in range(t)) + (2 + parts) * it
                if not isinstance(it, int) or TURNS * t + it > 0:
                    eng.wait_ge(att_ready, it + TURNS * t)
                eng.wait_ge(null_p, it + TURNS * t + 1)
                stand(eng, pool_passed)
                nc.gpsimd.tensor_tensor(den[:, :, :], pn[:, :, heads], rsum[:, r, 0, :, heads], ALU.add
                                        ).then_inc(normal_step, 1)
                eng.wait_ge(normal_step, done + 1)
                if parts > 1:
                    stand(eng, pool_passed)
                    nc.gpsimd.tensor_tensor(den[:, :, :], den[:, :, :], rsum[:, r, 1, :, heads], ALU.add
                                            ).then_inc(normal_step, 1)
                    eng.wait_ge(normal_step, done + 2)
                stand(eng, pool_passed)
                nc.gpsimd.tensor_scalar(den[:, :, :], den[:, :, :], PSCALE, None, ALU.mult).then_inc(den_ready, 1)
                nc.gpsimd.tensor_tensor(nullv[:, :, :, :], pn[:, :, heads].unsqueeze(3).broadcast_to([P, B, 4, DH]),
                                        nv[:, :].unsqueeze(1).unsqueeze(1).broadcast_to([P, B, 4, DH]), ALU.mult
                                        ).then_inc(normal_step, 1)
                eng.wait_ge(normal_step, done + parts + 1)
                o = att[:, r, :, heads, :]
                eng.wait_ge(o_out, 2 * it + 2 * TURNS * t + 2)
                stand(eng, pool_passed)
                nc.gpsimd.tensor_tensor(o, o, nullv[:, :, :, :], ALU.add).then_inc(normal_step, 1)
                eng.wait_ge(normal_step, done + parts + 2)
                eng.wait_ge(inverse_ready, it + TURNS * t + 1)
                stand(eng, pool_passed)
                nc.gpsimd.tensor_tensor(o, o, den[:, :, :].unsqueeze(3).broadcast_to([P, B, 4, DH]), ALU.mult
                                        ).then_inc(att_ready, 1)

            def rows_out(t):
                eng.wait_ge(yn_ready, t + 1)
                for b in range(B):
                    link(nc.gpsimd.tensor_tensor(y[:, b, :], y[:, b, :], gout[:, :], ALU.mult))
                    if b == 0:
                        eng.wait_ge(xres_in, 16 * (t + 1))
                    nc.gpsimd.tensor_tensor(y[:, b, :], y[:, b, :], xres[:, b, :], ALU.add).then_inc(y_ready, 1)

            def first_bias(t):
                eng.wait_ge(unit_free, number[t, "v", 0] + 1)
                null_starts(t, 0)
                for k in range(early_edges(t)):
                    edge(t, 0, k)

            x_std(0)
            def over_partitions(n, a, e):
                eng.wait_ge(maxes_ready, n)
                nc.gpsimd.partition_all_reduce(allmax[:, a:e], maxes[:, a:e], P, ABSMAX).then_inc(allmax_ready, 1)

            over_partitions(1, 0, 14)
            far = eng.to_reg(-FAR)
            eng.wait_ge(square_ready, 1)
            nc.gpsimd.tensor_tensor(sc[:, 2:3], sc[:, 1:2], powers[:, 0:1], ALU.pow).then_inc(root_ready, 1)
            for c in range(C):
                eng.wait_ge(wq_in[c], 16)
                if c == 0:
                    eng.wait_ge(small_in, 16 * 5)
                nc.gpsimd.tensor_tensor(tmp[:, c, :].rearrange("p (h d) -> p h d", d=DH),
                                        wq32[:, c, :].rearrange("p (h d) -> p h d", d=DH),
                                        nk.unsqueeze(1).broadcast_to([P, H, DH]), ALU.mult).then_inc(product_ready, 1)
            over_partitions(2, 14, 16)

            first_bias(0)
            for t in range(QT):
                def turn(it):
                    for k in range(early_edges(t), 4):
                        edge(t, it, k)
                    null_shifts(t, it)
                    if not isinstance(it, int) or it < TURNS - 1:
                        null_starts(t, it + 1)
                        for k in range(early_edges(t)):
                            edge(t, it + 1, k)
                    elif t + 1 < QT:
                        first_bias(t + 1)

                turn(0)
                if t == 0:
                    over_partitions(3, 16, 24)
                else:
                    normalise(t - 1, TURNS - 1)
                if t + 1 < QT:
                    x_std(t + 1)
                with eng.Fori(1, TURNS - PEELED) as it:
                    turn(it)
                    normalise(t, it - 1)
                if t > 1:
                    rows_out(t - 2)
                for it in range(TURNS - PEELED, TURNS):
                    turn(it)
                    normalise(t, it - 1)
                if t > 0:
                    y_std(t - 1)
            normalise(QT - 1, TURNS - 1)
            rows_out(QT - 2)
            for b in range(B):
                y_std(QT - 1, b)

        @block.tensor
        def _(eng):
            def unit(n):
                if not isinstance(n, int) or n >= TP:
                    eng.wait_ge(unit_free, n - TP + 1)

            def products(dst, pairs):
                for i, (a, m) in enumerate(pairs):
                    ins = nc.tensor.matmul(dst, a, m, start=i == 0, stop=i == len(pairs) - 1, skip_group_check=True)
                return ins

            def other(t, kind, i):
                n = number[t, kind, i]
                dst = tp[:, n % TP, :]
                unit(n)
                if kind == "x":
                    eng.wait_ge(xn_ready, B * t + i + 1)
                    for c in range(C):
                        ins = nc.tensor.transpose(dst[:, c * P:(c + 1) * P], xin[:, i, c * P:(c + 1) * P], ident[:, :])
                elif kind == "q":
                    if i == 0:
                        eng.wait_ge(unit_free, number[t, "x", B - 1] + 1)
                        if t == 0:
                            eng.wait_ge(weights_ready, 1)
                    w = slice(i * P, (i + 1) * P)
                    ins = products(dst[:, 0:B * P],
                                   [(wqs[:, c, w], xs[:, c, :, :].rearrange("p b q -> p (b q)"))
                                    for c in range(C) for wqs, xs in ((wqh, xth), (wqh, xtl), (wql, xth))])
                elif kind == "k":
                    if t == 0:
                        eng.wait_ge(weights_ready, 2)
                    ins = products(dst[:, 0:B * P],
                                   [(ws[:, c, :, :].rearrange("p a d -> p (a d)"),
                                     xs[:, c, :, :].rearrange("p b q -> p (b q)"))
                                    for c in range(C) for ws, xs in ((wkh, xth), (wkh, xtl), (wkl, xth))])
                elif kind == "v":
                    if t == 0:
                        eng.wait_ge(weights_ready, 3)
                    for b in range(B):
                        ins = products(dst[:, b * P:b * P + NSN],
                                       [(xs[:, c, b, :], ws[:, c, :])
                                        for c in range(C) for ws, xs in ((wvh, xth), (wvh, xtl), (wvl, xth))])
                elif kind == "att":
                    if i == 0:
                        eng.wait_ge(att_ready, TURNS * (t + 1))
                    rows = att[:, t % 2, :, :, :].rearrange("p b h d -> p (b h d)")
                    for c in range(GROUP):
                        at = (GROUP * i + c) * P
                        ins = nc.tensor.transpose(dst[:, c * P:(c + 1) * P], rows[:, at:at + P], ident[:, :])
                else:
                    b, cols = i // 2, slice(i % 2 * D // 2, (i % 2 + 1) * D // 2)
                    eng.wait_ge(unit_free, number[t, "att", 2 * b + 1] + 1)
                    if t == 0 and i == 0:
                        eng.wait_ge(wo_ready, 4)
                    ins = products(dst[:, 0:D // 2],
                                   [(a[:, b, c, :], w[:, c, cols])
                                    for c in range(CO) for a, w in ((ath, woh), (ath, wol), (atl, woh))])
                ins.then_inc(unit_full, 1)

            def scores(t, it, f):
                it, f, j, ck = locate(t, it, f)
                h = 4 * it + j // 2
                a, e = chunk(t, ck)
                n = group_of(t, it, f)
                if not isinstance(n, int) or n > 1:
                    eng.wait_ge(biased, n - 1)
                dst = sp[:, f % 2, 0:e - a]
                nc.tensor.matmul(dst, qa[:, t % 2, h, j % 2, :], k1[:, j % 2, a:e], start=True, stop=False,
                                 skip_group_check=True)
                nc.tensor.matmul(dst, qb[0:DH + 1, t % 2, h, j % 2, :], k2[0:DH + 1, j % 2, a:e], start=False,
                                 stop=True, skip_group_check=True).then_inc(scores_full, 1)

            def turn_p(t, it, f):
                it, f, j, g = locate(t, it, f)
                unit(unit_of(t, it, f))
                if g % 2 == 0:
                    eng.wait_ge(exp_done, exp_at[t] + exps(t) * (BODY * it + j) + g // 2 + 1)
                for i, kb in enumerate(groups(t)[g]):
                    ins = nc.tensor.transpose(tp[:, slot_of(t, it, f), i * P:(i + 1) * P],
                                              ps[:, j % 4, kb * P:(kb + 1) * P], ident[:, :])
                ins.then_inc(unit_full, 1)

            def times_v(t, it, f):
                it, f, j, g = locate(t, it, f)
                eng.wait_ge(unit_free, unit_of(t, it, f) + 1)
                if g == 0 and j % 4 == 0:
                    n = t * (STEPS // 4) + 2 * it + j // 4
                    if not isinstance(n, int) or n > 1:
                        eng.wait_ge(o_out, n - 1)
                dst = op[:, j // 4, (j % 4) * DH:(j % 4 + 1) * DH]
                for i, kb in enumerate(groups(t)[g]):
                    a = slice(i * P, (i + 1) * P)
                    nc.tensor.matmul(dst, pth[:, f % 4, a], v[:, kb, j % 2, 0, :], start=kb == 0, stop=False,
                                     skip_group_check=True)
                    nc.tensor.matmul(dst, pth[:, f % 4, a], v[:, kb, j % 2, 1, :], start=False, stop=False,
                                     skip_group_check=True)
                    ins = nc.tensor.matmul(dst, ptl[:, f % 4, a], v[:, kb, j % 2, 0, :], start=False, stop=kb == t,
                                           skip_group_check=True)
                ins.then_inc(pv_done, 1)

            def queries_ready(t):
                eng.wait_ge(qb_in, 16 * (t + 1))
                eng.wait_ge(unit_free, number[t, "k", 0] + 1)

            eng.wait_ge(ident_ready, 1)
            for kind, i in PROLOGUE:
                other(0, kind, i)
            for t in range(QT):
                if t == 0:
                    queries_ready(0)
                    for n in range(scored(0)):
                        scores(0, 0, n)

                def first():
                    for f in range(AHEAD):
                        turn_p(t, 0, f)
                        scores(t, 0, scored(t) + f)

                def next_scores(n):
                    if n == 0:
                        queries_ready(t + 1)
                    scores(t + 1, 0, n)

                def turn(it):
                    ahead = look_ahead(t, it, lambda it, f: scores(t, it, f), next_scores)
                    for f in range(BODY * len(groups(t))):
                        if here(it, f + AHEAD, t):
                            turn_p(t, it, f + AHEAD)
                        ahead(f)
                        times_v(t, it, f)
                        for tile, kind, i in units_beside(t, it, f):
                            other(tile, kind, i)

                tile_loop(eng, t, first, turn)
            for kind, i in EPILOGUE:
                other(QT - 1, kind, i)

        @block.scalar
        def _(eng):
            def small(dst, src):
                eng.dma_start(dst, src).then_inc(small_in, 16)

            small(gcol[:, :], g_in)
            small(nk[:, :], bc(cond[0], DH))
            small(nv[:, :], bc(cond[1], DH))
            small(nb[:, :], bc(null_bias, H))
            small(gout[:, :], bc(g_out, D))
            eng.dma_start(mask8[DH:DH + 1, :, :], mask.rearrange("(a b) n -> a b n", a=1)).then_inc(mask_in, 16)

            def high(dst, src, scale=1.0):
                return nc.scalar.activation(dst, src, ACT.Copy, scale=scale)

            def other(t, kind, i):
                n = number[t, kind, i]
                src = tp[:, n % TP, :]
                if kind == "k":
                    eng.wait_ge(unit_high, number[t, "q", UQ - 1] + 1)
                    eng.dma_start(qb[0:DH, t % 2, :, :, :], qa[0:DH, t % 2, :, :, :]).then_inc(qb_in, 16)
                if kind == "out" and 0 < t < QT - 1:
                    eng.wait_ge(y_out, 16 * t)
                eng.wait_ge(unit_full, n + 1)
                if kind == "x":
                    ins = high(xth[:, :, i, :], src.rearrange("p (c q) -> p c q", c=C))
                elif kind == "q":
                    for odd in range(2):
                        ins = high(qa[0:DH, t % 2, 2 * i + odd, :, :],
                                   src[DH * odd:DH * odd + DH, 0:B * P].rearrange("p (b q) -> p b q", b=B))
                elif kind == "k":
                    ins = high(k1[:, :, t * P:(t + 1) * P], src[:, 0:B * P].rearrange("p (b q) -> p b q", b=B))
                elif kind == "v":
                    ins = high(v[:, t, :, 0, :], src[:, 0:B * P].rearrange("p (b q) -> p b q", b=B)[:, :, 0:DH])
                elif kind == "att":
                    c0 = GROUP * (i % 2)
                    ins = high(ath[:, i // 2, c0:c0 + GROUP, :], src.rearrange("p (c q) -> p c q", c=GROUP))
                else:
                    ins = high(rows_of[t][:, i // 2, i % 2 * D // 2:(i % 2 + 1) * D // 2], src[:, 0:D // 2])
                ins.then_inc(unit_high, 1)

            def null_weights(t, it):
                eng.wait_ge(null_shift, it + TURNS * t + 1)
                w = pn[:, :, span(4 * it, 4)]
                nc.scalar.activation(w, w, ACT.Exp).then_inc(null_p, 1)

            def exp(t, it, j, c):
                it, j = it + j // BODY, j % BODY
                G, h = len(groups(t)), 4 * it + j // 2
                if c == 0:
                    eng.wait_ge(biased, group_of(t, it, G * (j + 1)))
                a, e = chunk(t, c, EXP)
                nc.scalar.activation(ps[:, j % 4, a:e], ps[:, j % 4, a:e], ACT.Exp, bias=rowmin[:, j, G - 1:G],
                                     scale=-1.0, accum_out=rsum[:, t % 2, c, j % 2, span(h, 1)]
                                     ).then_inc(exp_done, 1)

            def p_high(t, it, f):
                it, f, j, g = locate(t, it, f)
                eng.wait_ge(unit_full, unit_of(t, it, f) + 1)
                n = group_of(t, it, f)
                if not isinstance(n, int) or n > 3:
                    eng.wait_ge(pv_done, n - 3)
                w = len(groups(t)[g]) * P
                high(pth[:, f % 4, 0:w], tp[:, slot_of(t, it, f), 0:w], PSCALE).then_inc(unit_high, 1)

            def take_o(t, it, j):
                eng.wait_ge(pv_done, group_of(t, it, len(groups(t)) * (j + 1)))
                h = 4 * it + 2 * (j // 4)
                for b in range(B):
                    ins = high(att[:, t % 2, b, span(h, 2), :],
                               op[:, j // 4, 0:4 * DH].rearrange("p (h b d) -> p h b d", h=2, b=B)[:, :, b, :])
                ins.then_inc(o_out, 1)

            def first_exps(t):
                for j in range(lead(t)):
                    for c in range(exps(t)):
                        exp(t, 0, j, c)

            def next_exps(t):
                G = len(groups(t))
                own = (BODY - lead(t)) * G - 1 - AHEAD
                with_bias = BODY * G - AHEAD - scored(t) + lead(t + 1) * len(groups(t + 1))
                return min(max(own, with_bias), BODY * G - 1)

            def weights_high():
                eng.wait_ge(scales_ready, 1)
                for c in range(C):
                    nc.scalar.activation(wqh[:, c, :], wq32[:, c, :], ACT.Copy, scale=gq[:, c:c + 1]
                                         ).then_inc(whigh_ready, 1)
                for a in range(2):
                    ins = high(wkh[:, :, a, :], wkv32[:, :, 0:DH], sc[:, 2:3])
                ins.then_inc(whigh_ready, 1)
                high(wvh[:, :, 0:DH], wkv32[:, :, DH:2 * DH], sc[:, 4:5])
                eng.wait_ge(scales_ready, 2)
                high(wvh[:, :, DH:NSN], wn32, sc[:, 5:6]).then_inc(whigh_ready, 1)

            def wo_high(k):
                if k == 0:
                    eng.wait_ge(scales_ready, 3)
                high(woh[:, 2 * k:2 * k + 2, :], wo32[:, k, :].rearrange("p (c n) -> p c n", n=D), sc[:, 7:8]
                     ).then_inc(whigh_ready, 1)

            for kind, i in PROLOGUE:
                if (kind, i) == ("q", 0):
                    weights_high()
                other(0, kind, i)
            for t in range(QT):
                G = len(groups(t))
                if t == 0:
                    first_exps(0)

                def group(it, f):
                    p_high(t, it, f)
                    it, f, j, g = locate(t, it, f)
                    if g % 2 == 0 and here(it, f + lead(t) * G, t):
                        exp(t, it, j + lead(t), g // 2)

                def first():
                    for f in range(AHEAD):
                        group(0, f)

                def turn(it):
                    last = isinstance(it, int) and it == TURNS - 1
                    for f in range(BODY * G):
                        if here(it, f + AHEAD, t):
                            group(it, f + AHEAD)
                        if last and t + 1 < QT and f == next_exps(t):
                            first_exps(t + 1)
                        if f == 4 * G + 1:
                            take_o(t, it, 3)
                        if t == 0 and isinstance(it, int) and it == TURNS - PEELED and f % 2 == 1:
                            wo_high(f // 2)
                        for tile, kind, i in units_beside(t, it, f):
                            other(tile, kind, i)
                    null_weights(t, it)
                    take_o(t, it, 7)

                tile_loop(eng, t, first, turn)
            for kind, i in EPILOGUE:
                other(QT - 1, kind, i)

        @block.vector
        def _(eng):
            links = [0]

            def link(ins):
                links[0] += 1
                ins.then_inc(dve_link, 1)
                eng.wait_ge(dve_link, links[0])

            def low(dst, src, hi_half, scale=1.0):
                return nc.vector.scalar_tensor_tensor(out=dst, in0=src, scalar=scale, in1=hi_half, op0=ALU.mult,
                                                      op1=ALU.subtract)

            def col(k):
                return sc[:, k:k + 1]

            def largest(k, a):
                nc.vector.tensor_reduce(maxes[:, k:k + 1], a, mybir.AxisListType.XY, ALU.max)
                return nc.vector.tensor_reduce(maxes[:, k + 1:k + 2], a, mybir.AxisListType.XY, ALU.min)

            def of_all(dst, a):
                link(nc.vector.tensor_reduce(dst, a, AX_X, ALU.max))
                link(nc.vector.tensor_scalar(dst, dst, 1e-18, None, ALU.max))

            def weight_maxes():
                eng.wait_ge(small_in, 16 * 5)
                eng.wait_ge(wkv_in, 16)
                for c in range(C):
                    ins = nc.vector.tensor_scalar(wkv32[:, c, :], wkv32[:, c, :], gcol[:, c:c + 1], None, ALU.mult)
                link(ins)
                largest(8, wkv32[:, :, 0:DH])
                largest(10, wkv32[:, :, DH:2 * DH])
                largest(12, nv[:, :].unsqueeze(1))
                for c in range(C):
                    eng.wait_ge(wq_in[c], 16)
                    nc.vector.tensor_reduce(maxes[:, c:c + 1], wq32[:, c, :], AX_X, ALU.max)
                    ins = nc.vector.tensor_reduce(maxes[:, C + c:C + c + 1], wq32[:, c, :], AX_X, ALU.min)
                link(ins)
                nc.vector.tensor_tensor(maxes[:, 0:2 * C].rearrange("p (a c) -> p a c", c=C),
                                        maxes[:, 0:2 * C].rearrange("p (a c) -> p a c", c=C),
                                        gcol[:, :].unsqueeze(1).broadcast_to([P, 2, C]), ALU.mult
                                        ).then_inc(maxes_ready, 1)

            def scales():
                eng.wait_ge(allmax_ready, 1)
                of_all(sc[:, 9:10], allmax[:, 0:8])
                of_all(sc[:, 10:13], allmax[:, 8:14].rearrange("p (k e) -> p k e", e=2))
                aq, ak, av, anv = (col(k) for k in range(9, 13))
                link(nc.vector.reciprocal(col(0), ak))
                nc.vector.tensor_scalar(col(1), col(0), aq, DH ** -0.5, ALU.mult, ALU.mult).then_inc(square_ready, 1)
                link(nc.vector.tensor_scalar(col(4), anv, 1.0 / D, av, ALU.mult, ALU.max))
                link(nc.vector.reciprocal(col(4), col(4)))
                link(nc.vector.tensor_scalar(col(4), col(4), 16.0, None, ALU.mult))
                nc.vector.tensor_scalar(nv[:, :], nv[:, :], col(4), PSCALE, ALU.mult, ALU.mult)
                eng.wait_ge(root_ready, 1)
                link(nc.vector.reciprocal(col(3), col(2)))
                link(nc.vector.tensor_scalar(col(3), col(3), DH ** -0.5, None, ALU.mult))
                nc.vector.tensor_scalar(gq[:, :], gcol[:, :], col(3), None, ALU.mult).then_inc(scales_ready, 1)

            def weights_low():
                for c in range(C):
                    eng.wait_ge(whigh_ready, c + 1)
                    ins = low(wql[:, c, :], wq32[:, c, :], wqh[:, c, :], gq[:, c:c + 1])
                ins.then_inc(weights_ready, 1)
                eng.wait_ge(whigh_ready, C + 1)
                for a in range(2):
                    ins = low(wkl[:, :, a, :], wkv32[:, :, 0:DH], wkh[:, :, a, :], col(2))
                ins.then_inc(weights_ready, 1)
                for c in range(C):
                    eng.wait_ge(product_ready, c + 1)
                    ins = nc.vector.tensor_reduce(wn32[:, c, :], tmp[:, c, :].rearrange("p (h d) -> p h d", d=DH),
                                                  AX_X, ALU.add)
                link(ins)
                for c in range(C):
                    ins = nc.vector.tensor_scalar(wn32[:, c, :], wn32[:, c, :], gcol[:, c:c + 1], DH ** -0.5,
                                                  ALU.mult, ALU.mult)
                link(ins)
                largest(14, wn32).then_inc(maxes_ready, 1)
                eng.wait_ge(allmax_ready, 2)
                of_all(col(13), allmax[:, 14:16])
                link(nc.vector.reciprocal(col(5), col(13)))
                nc.vector.tensor_scalar(col(6), col(13), -1.0 / 16.0, None, ALU.mult)
                nc.vector.tensor_scalar(col(5), col(5), 16.0, None, ALU.mult
                                        ).then_inc(scales_ready, 1)
                eng.wait_ge(scales_ready, 2)
                eng.wait_ge(whigh_ready, C + 2)
                low(wvl[:, :, 0:DH], wkv32[:, :, DH:2 * DH], wvh[:, :, 0:DH], col(4))
                low(wvl[:, :, DH:NSN], wn32, wvh[:, :, DH:NSN], col(5)).then_inc(weights_ready, 1)
                eng.wait_ge(mask_in, 16)
                nc.vector.tensor_scalar(k2[DH:DH + 1, :, :], mask8[DH:DH + 1, :, :], -1.0, MASK_FAR, ALU.add, ALU.mult)

            def wo_maxes(k):
                if k == 0:
                    eng.wait_ge(wo_in, 16 * 4)
                ins = largest(16 + 2 * k, wo32[:, k, :].unsqueeze(1))
                if k == 3:
                    ins.then_inc(maxes_ready, 1)

            def wo_scales():
                eng.wait_ge(allmax_ready, 3)
                of_all(col(14), allmax[:, 16:24])
                link(nc.vector.reciprocal(col(7), col(14)))
                link(nc.vector.tensor_scalar(col(7), col(7), 1024.0, None, ALU.mult))
                link(nc.vector.tensor_scalar(col(8), col(4), col(7), None, ALU.mult))
                nc.vector.tensor_scalar(col(8), col(8), col(8), EPS, ALU.mult, ALU.mult).then_inc(scales_ready, 1)

            def wo_low(k):
                eng.wait_ge(whigh_ready, C + 3 + k)
                low(wol[:, 2 * k:2 * k + 2, :], wo32[:, k, :].rearrange("p (c n) -> p c n", n=D),
                    woh[:, 2 * k:2 * k + 2, :], col(7)).then_inc(wo_ready, 1)

            def moments(dst, b, src):
                link(nc.vector.bn_stats(st[:, b, 0:6], src))
                return nc.vector.bn_aggr(dst[:, b, :], st[:, b, 0:6])

            def moments_x(t):
                eng.wait_ge(x_in, 16 * (t + 1))
                for b in range(B):
                    ins = moments(xst, b, xin[:, b, :])
                ins.then_inc(xvar_ready, 1)

            def norm_rows(a, b, mv):
                return nc.vector.tensor_scalar(a, a, mv[:, b, 0:1], mv[:, b, 1:2], ALU.subtract, ALU.mult)

            def norm_x(t):
                eng.wait_ge(xstd_ready, t + 1)
                for b in range(B):
                    norm_rows(xin[:, b, :], b, xst).then_inc(xn_ready, 1)

            def norm_y(t):
                eng.wait_ge(ystd_ready, t + 1)
                for b in range(B):
                    ins = norm_rows(y[:, b, :], b, yst)
                ins.then_inc(yn_ready, 1)

            def last_rows(b):
                rows = rows_of[QT - 1][:, b, :]
                eng.wait_ge(ystd_ready, QT + b)
                link(norm_rows(rows, b, yst))
                link(nc.vector.tensor_tensor(rows, rows, gout[:, :], ALU.mult))
                if b == 0:
                    eng.wait_ge(xres_in, 16 * QT)
                nc.vector.tensor_tensor(rows, rows, xres[:, b, :], ALU.add).then_inc(y_ready, 1)

            def other(t, kind, i):
                n = number[t, kind, i]
                src = tp[:, n % TP, :]
                eng.wait_ge(unit_high, n + 1)
                if kind == "x":
                    ins = low(xtl[:, :, i, :], src.rearrange("p (c q) -> p c q", c=C), xth[:, :, i, :])
                elif kind == "q":
                    for odd in range(2):
                        ins = low(qa[DH:P, t % 2, 2 * i + odd, :, :],
                                  src[DH * odd:DH * odd + DH, 0:B * P].rearrange("p (b q) -> p b q", b=B),
                                  qa[0:DH, t % 2, 2 * i + odd, :, :])
                elif kind == "k":
                    ins = low(k2[0:DH, :, t * P:(t + 1) * P], src[0:DH, 0:B * P].rearrange("p (b q) -> p b q", b=B),
                              k1[0:DH, :, t * P:(t + 1) * P])
                elif kind == "v":
                    vals = src[:, 0:B * P].rearrange("p (b q) -> p b q", b=B)
                    low(v[:, t, :, 1, :], vals[:, :, 0:DH], v[:, t, :, 0, :])
                    ins = nc.vector.scalar_tensor_tensor(
                        out=nsn[:, t % 3, :, :], in0=vals[:, :, DH:NSN], scalar=sc[:, 6:7],
                        in1=nb[:, :].unsqueeze(1).broadcast_to([P, B, H]), op0=ALU.mult, op1=ALU.subtract)
                elif kind == "att":
                    c0 = GROUP * (i % 2)
                    ins = low(atl[:, i // 2, c0:c0 + GROUP, :], src.rearrange("p (c q) -> p c q", c=GROUP),
                              ath[:, i // 2, c0:c0 + GROUP, :])
                else:
                    b = i // 2
                    ins = nc.vector.bn_stats(yhalf[:, b, i % 2, :], src[:, 0:D // 2])
                    if i % 2 == 1:
                        link(ins)
                        ins = nc.vector.bn_aggr(yst[:, b, :], yhalf[:, b, :, :].rearrange("p a s -> p (a s)"))
                ins.then_inc(unit_free, 1)

            def inverses(n):
                eng.wait_ge(den_ready, n)
                nc.vector.reciprocal(den[:, :, :], den[:, :, :]).then_inc(inverse_ready, 1)

            def add_bias(t, it, f):
                it, f, j, ck = locate(t, it, f)
                n = group_of(t, it, f)
                eng.wait_ge(scores_full, n + 1)
                if ck == 0:
                    if j % 2 == 0:
                        eng.wait_ge(bias_ready, H * t + 4 * it + j // 2 + 1)
                    if j == 0:
                        eng.wait_ge(start_ready, TURNS * t + it + 1)
                    least = start[:, j:j + 1]
                else:
                    eng.wait_ge(biased, n)
                    least = rowmin[:, j, ck - 1:ck]
                stand(eng, dve_passed)
                a, e = chunk(t, ck)
                nc.vector.tensor_tensor_reduce(ps[:, j % 4, a:e], sp[:, f % 2, 0:e - a], bias_row(t, j // 2, a, e),
                                               -1.0, least, ALU.add, ALU.min, rowmin[:, j, ck:ck + 1]
                                               ).then_inc(biased, 1)

            def p_low(t, it, f):
                it, f, j, g = locate(t, it, f)
                eng.wait_ge(unit_high, unit_of(t, it, f) + 1)
                w = len(groups(t)[g]) * P
                low(ptl[:, f % 4, 0:w], tp[:, slot_of(t, it, f), 0:w], pth[:, f % 4, 0:w], PSCALE
                    ).then_inc(unit_free, 1)

            nc.vector.memset(maxes[:, :], 0.0)
            nc.vector.memset(rowmin[:, :, :], 0.0)
            moments_x(0)
            weight_maxes()
            norm_x(0)
            for kind, i in PROLOGUE:
                if (kind, i) == ("q", 0):
                    scales()
                    weights_low()
                other(0, kind, i)
            for t in range(QT):
                G = len(groups(t))
                if t == 0:
                    for n in range(scored(0)):
                        add_bias(0, 0, n)

                def first():
                    if t + 1 < QT:
                        moments_x(t + 1)
                    for f in range(AHEAD):
                        p_low(t, 0, f)
                        add_bias(t, 0, scored(t) + f)
                    if t > 1:
                        norm_y(t - 2)

                def turn(it):
                    if isinstance(it, int) and it == TURNS - PEELED and t + 1 < QT:
                        norm_x(t + 1)
                        if t == 0:
                            wo_scales()
                    ahead = look_ahead(t, it, lambda it, f: add_bias(t, it, f), lambda n: add_bias(t + 1, 0, n))
                    for f in range(BODY * G):
                        ahead(f)
                        if here(it, f + AHEAD, t):
                            p_low(t, it, f + AHEAD)
                        if f == min(BODY * G - AHEAD - scored(t) + 5, BODY * G - 1) and (
                                not isinstance(it, int) or TURNS * t + it > 0):
                            inverses(it + TURNS * t)
                        if t == 0 and isinstance(it, int) and f % 2 == 1:
                            if it == 0:
                                wo_maxes(f // 2)
                            elif it == TURNS - PEELED:
                                wo_low(f // 2)
                        for tile, kind, i in units_beside(t, it, f):
                            other(tile, kind, i)

                tile_loop(eng, t, first, turn)
            norm_y(QT - 2)
            inverses(TURNS * QT)
            for kind, i in EPILOGUE:
                other(QT - 1, kind, i)
                if kind == "out" and i % 2 == 1:
                    last_rows(i // 2)


_INS = ['x', 'fside_16xSxS_0', 'cond_64', 'mask_BxS_bk0', 'L0_cond_g_in', 'L0_cond_null_attn_bias', 'L0_cond_Wq',
        'L0_cond_Wkv', 'L0_cond_Wo', 'L0_cond_g_out']


def kernel(**inputs):
    import numpy as np
    import concourse.bacc as bacc
    from concourse.bass_utils import run_bass_kernel_spmd

    nc = bacc.Bacc("TRN2", target_bir_lowering=False, num_devices=1)
    arrays, args = {}, []
    for name in _INS:
        a = np.ascontiguousarray(inputs[name])
        if name == 'L0_cond_g_in':
            a = np.ascontiguousarray(a.reshape(-1, P).T)
        arrays[f"in_{name}"] = a
        args.append(nc.dram_tensor(f"in_{name}", a.shape, mybir.dt.from_np(a.dtype), kind="ExternalInput").ap())
    out = nc.dram_tensor("out", arrays["in_x"].shape, F32, kind="ExternalOutput").ap()
    cond_attention(nc, *args, out)
    r = run_bass_kernel_spmd(nc, [arrays], core_ids=[0])
    return r.results[0]["out"]
```
